# Optimizing a Trainium2 kernel written in Bass

```python
import numpy as np
import jax
import jax.numpy as jnp

def _softmax(x, axis=-1):
    return jax.nn.softmax(x, axis=axis)

def _gelu(x):
    return jax.nn.gelu(x, approximate=True)

def _silu(x):
    return jax.nn.silu(x)

def _sigmoid(x):
    return jax.nn.sigmoid(x)

def _layernorm(x, axis=-1, eps=1e-05):
    m = jnp.mean(x, axis=axis, keepdims=True)
    v = jnp.var(x, axis=axis, keepdims=True)
    return (x - m) / jnp.sqrt(v + eps)

def _scatter_add(tgt, idx, src, axis=0):
    return tgt.at[idx].add(src)

def _segment_sum(src, seg, n):
    return jax.ops.segment_sum(src, seg, n)
kernel_name = 'mk_flamingo_gated_d1_seqx_r4_93889f'

def setup_inputs(seed: int=0):
    np.random.seed(seed)
    _w = jnp.asarray

    def _rec_inputs():
        import jax
        import jax.numpy as jnp
        _rk = jax.random.key(seed)
        x = -0.0002928 + 1 * jax.random.normal(jax.random.fold_in(_rk, 1), (32, 112, 256), jnp.float32)
        _lenS = 112 - jax.random.randint(jax.random.fold_in(_rk, 7), (32,), 0, max(1, 112 // 4) + 1, jnp.int32)
        _lenS2 = 375 - jax.random.randint(jax.random.fold_in(_rk, 8), (32,), 0, max(1, 375 // 4) + 1, jnp.int32)
        _ctx_512P = jax.random.normal(jax.random.fold_in(_rk, 11), (32, 16, 128), jnp.float32)
        _ctx_512c = jax.random.dirichlet(jax.random.fold_in(_rk, 511), 0.3 * jnp.ones((16,), jnp.float32), (32, 375))
        _ctx_512t = jnp.einsum('bsk,bkd->bsd', _ctx_512c, _ctx_512P)
        _ctx_512t = _ctx_512t * jax.lax.rsqrt(jnp.mean(jnp.square(_ctx_512t)) + 1e-12) * 0.953939
        ctx_512 = -1.52775e-05 + 0.999936 * (_ctx_512t + 0.3 * jax.random.normal(jax.random.fold_in(_rk, 611), (32, 375, 128), jnp.float32))
        _g = jax.random.normal(jax.random.fold_in(_rk, 9001), (2, 1), jnp.float32)
        _g = jnp.sign(_g) * jnp.maximum(jnp.abs(_g), 1.0) + (_g == 0) * 1.0
        g_xattn = _g[0]
        g_ffn = _g[1]
        return (x, ctx_512, g_xattn, g_ffn)
    x, ctx_512, g_xattn, g_ffn = _rec_inputs()

    def _L0_xattn_setup():
        import jax, jax.numpy as jnp
        import numpy as np
        NUM_HEADS = 16
        HEAD_DIM = 64
        Q_DIM = 256
        KV_DIM = 128
        INNER = NUM_HEADS * HEAD_DIM
        key = jax.random.key(seed)
        ks = jax.random.split(key, 7)
        B, N, M = (32, 128, 512)
        q = jax.random.normal(ks[0], (B, N, Q_DIM), dtype=jnp.float32)
        kv = jax.random.normal(ks[1], (B, M, KV_DIM), dtype=jnp.float32)
        Wq = jax.random.normal(ks[2], (Q_DIM, INNER), dtype=jnp.float32) / np.sqrt(Q_DIM)
        Wk = jax.random.normal(ks[3], (KV_DIM, INNER), dtype=jnp.float32) / np.sqrt(KV_DIM)
        Wv = jax.random.normal(ks[4], (KV_DIM, INNER), dtype=jnp.float32) / np.sqrt(KV_DIM)
        Wo = jax.random.normal(ks[5], (INNER, Q_DIM), dtype=jnp.float32) / np.sqrt(INNER)
        bo = jax.random.normal(ks[6], (Q_DIM,), dtype=jnp.float32) * 0.01
        return {'q': q, 'kv': kv, 'Wq': Wq, 'Wk': Wk, 'Wv': Wv, 'Wo': Wo, 'bo': bo}
    _L0_xattn_all = _L0_xattn_setup()
    _L0_xattn_in = {k: v for k, v in _L0_xattn_all.items() if k in ('Wq', 'Wk', 'Wv', 'Wo', 'bo')}
    del _L0_xattn_all

    def _L0_ffn_setup():
        import jax, jax.numpy as jnp
        import numpy as np
        D_MODEL = 256
        HIDDEN = 512
        E_ROUTED = 14
        E_SHARED = 2
        TOP_K = 2
        EPS = 1e-09
        RMS_EPS = 1.1920929e-07

        def _ffn(xn, rw, W1, W2):
            ms = jnp.mean(xn * xn, axis=-1, keepdims=True)
            h = xn * jax.lax.rsqrt(ms + RMS_EPS) * rw
            return jax.nn.silu(h @ W1) @ W2
        key = jax.random.key(seed)
        ks = jax.random.split(key, 9)
        B, T = (2, 256)
        x = jax.random.normal(ks[0], (B, T, D_MODEL), dtype=jnp.float32)
        router_w = jax.random.normal(ks[1], (D_MODEL, E_ROUTED), dtype=jnp.float32) * 0.006
        rms_w = jnp.ones((E_ROUTED, D_MODEL), dtype=jnp.float32)
        w1 = jax.random.normal(ks[2], (E_ROUTED, D_MODEL, HIDDEN), dtype=jnp.float32) * 0.02
        w2 = jax.random.normal(ks[3], (E_ROUTED, HIDDEN, D_MODEL), dtype=jnp.float32) * 0.02
        rms_w_s = jnp.ones((E_SHARED, D_MODEL), dtype=jnp.float32)
        w1_s = jax.random.normal(ks[4], (E_SHARED, D_MODEL, HIDDEN), dtype=jnp.float32) * 0.02
        w2_s = jax.random.normal(ks[5], (E_SHARED, HIDDEN, D_MODEL), dtype=jnp.float32) * 0.02
        return {'x': x, 'router_w': router_w, 'rms_w': rms_w, 'w1': w1, 'w2': w2, 'rms_w_s': rms_w_s, 'w1_s': w1_s, 'w2_s': w2_s}
    _L0_ffn_all = _L0_ffn_setup()
    _L0_ffn_in = {k: v for k, v in _L0_ffn_all.items() if k in ('router_w', 'rms_w', 'w1', 'w2', 'rms_w_s', 'w1_s', 'w2_s')}
    del _L0_ffn_all
    return {'x': x, 'ctx_512': ctx_512, 'g_xattn': g_xattn, 'g_ffn': g_ffn, 'L0_xattn_Wq': _L0_xattn_in['Wq'], 'L0_xattn_Wk': _L0_xattn_in['Wk'], 'L0_xattn_Wv': _L0_xattn_in['Wv'], 'L0_xattn_Wo': _L0_xattn_in['Wo'], 'L0_xattn_bo': _L0_xattn_in['bo'], 'L0_ffn_router_w': _L0_ffn_in['router_w'], 'L0_ffn_rms_w': _L0_ffn_in['rms_w'], 'L0_ffn_w1': _L0_ffn_in['w1'], 'L0_ffn_w2': _L0_ffn_in['w2'], 'L0_ffn_rms_w_s': _L0_ffn_in['rms_w_s'], 'L0_ffn_w1_s': _L0_ffn_in['w1_s'], 'L0_ffn_w2_s': _L0_ffn_in['w2_s']}

def reference(x, ctx_512, g_xattn, g_ffn, L0_xattn_Wq, L0_xattn_Wk, L0_xattn_Wv, L0_xattn_Wo, L0_xattn_bo, L0_ffn_router_w, L0_ffn_rms_w, L0_ffn_w1, L0_ffn_w2, L0_ffn_rms_w_s, L0_ffn_w1_s, L0_ffn_w2_s):
    import jax
    import jax.numpy as jnp

    def _L0_xattn_ref(q, kv, Wq, Wk, Wv, Wo, bo):
        import jax, jax.numpy as jnp
        import numpy as np
        NUM_HEADS = 16
        HEAD_DIM = 64
        Q_DIM = 256
        KV_DIM = 128
        INNER = NUM_HEADS * HEAD_DIM
        B, N, _ = q.shape
        M = kv.shape[1]
        scale = HEAD_DIM ** (-0.5)
        qh = (q @ Wq).reshape(B, N, NUM_HEADS, HEAD_DIM).transpose(0, 2, 1, 3)
        kh = (kv @ Wk).reshape(B, M, NUM_HEADS, HEAD_DIM).transpose(0, 2, 1, 3)
        vh = (kv @ Wv).reshape(B, M, NUM_HEADS, HEAD_DIM).transpose(0, 2, 1, 3)
        scores = jnp.einsum('bhnd,bhmd->bhnm', qh, kh) * scale
        attn = jax.nn.softmax(scores, axis=-1)
        out = jnp.einsum('bhnm,bhmd->bhnd', attn, vh)
        out = out.transpose(0, 2, 1, 3).reshape(B, N, INNER)
        return out @ Wo + bo

    def _L0_ffn_ref(x, router_w, rms_w, w1, w2, rms_w_s, w1_s, w2_s):
        import jax, jax.numpy as jnp
        import numpy as np
        D_MODEL = 256
        HIDDEN = 512
        E_ROUTED = 14
        E_SHARED = 2
        TOP_K = 2
        EPS = 1e-09
        RMS_EPS = 1.1920929e-07

        def _ffn(xn, rw, W1, W2):
            ms = jnp.mean(xn * xn, axis=-1, keepdims=True)
            h = xn * jax.lax.rsqrt(ms + RMS_EPS) * rw
            return jax.nn.silu(h @ W1) @ W2
        B, T, D = x.shape
        N = B * T
        xf = x.reshape(N, D)
        gates = jax.nn.softmax(xf @ router_w, axis=-1)
        top_v, top_i = jax.lax.top_k(gates, TOP_K)
        masked = jnp.zeros_like(gates).at[jnp.arange(N)[:, None], top_i].set(top_v)
        masked = masked / (masked.sum(axis=-1, keepdims=True) + EPS)
        routed = jax.vmap(lambda rw_, W1_, W2_: _ffn(xf, rw_, W1_, W2_))(rms_w, w1, w2)
        routed_out = jnp.einsum('end,ne->nd', routed, masked)
        shared = jax.vmap(lambda rw_, W1_, W2_: _ffn(xf, rw_, W1_, W2_))(rms_w_s, w1_s, w2_s).sum(0)
        return (routed_out + shared).reshape(B, T, D)
    x = x + jnp.tanh(g_xattn[0]) * _L0_xattn_ref(_layernorm(x, axis=-1), ctx_512, L0_xattn_Wq, L0_xattn_Wk, L0_xattn_Wv, L0_xattn_Wo, L0_xattn_bo)
    x = x + jnp.tanh(g_ffn[0]) * _L0_ffn_ref(_layernorm(x, axis=-1), L0_ffn_router_w, L0_ffn_rms_w, L0_ffn_w1, L0_ffn_w2, L0_ffn_rms_w_s, L0_ffn_w1_s, L0_ffn_w2_s)
    return x

_drawn_inputs = setup_inputs


def setup_inputs(seed=0):
    import zlib

    import numpy as np

    out = dict(_drawn_inputs(seed))
    spreads = {'L0_ffn_rms_w': (1.0, 0.6), 'L0_ffn_rms_w_s': (1.0, 0.6)}
    factors = {'L0_xattn_bo': 6.723}
    for name, (base, spread) in spreads.items():
        noise = np.random.default_rng([zlib.crc32(name.encode()), seed]).standard_normal(out[name].shape)
        drawn = base * np.exp(spread * noise) if base else spread * noise
        out[name] = jnp.asarray(drawn.astype(out[name].dtype))
    for name, factor in factors.items():
        out[name] = (out[name] * factor).astype(out[name].dtype)
    return out
```

```python
from contextlib import ExitStack

import numpy as np

import concourse.bass as bass
from concourse import mybir

ALU = mybir.AluOpType
ACT = mybir.ActivationFunctionType
F32 = mybir.dt.float32
F32R = mybir.dt.float32r
I32 = mybir.dt.int32
U32 = mybir.dt.uint32
AX = mybir.AxisListType.X

P = 128
B, N, D = 32, 112, 256
M, C = 375, 128
MC, MP = 3, 125
MW = M + 1
H, HD = 16, 64
PAIRS = B // 2
HW_ROW = D + 1
E, HID, TOPK, SHARED = 14, 512, 2, 2
TOK = B * N
LN_EPS = 1e-5
RMS_EPS = 1.1920929e-07
TOP_EPS = 1e-9


def need(eng, sem, value):
    if isinstance(value, int) and value <= 0:
        return
    eng.wait_ge(sem, value)


def apart(eng):
    eng.nop(nofuse=True)


def fuse_weights(nc, io, sb, banks):
    with ExitStack() as ctx:
        def buf(name, shape, dt=F32):
            return ctx.enter_context(nc.sbuf_tensor(name, shape, dt))

        def sem(name):
            return ctx.enter_context(nc.semaphore(name))

        wq = buf("wq", [P, 2, H * HD])
        wk = buf("wk", [P, H * HD])
        wv = buf("wv", [P, H * HD])
        wo = buf("wo", [P, 8, D])
        wqT = buf("wqT", [P, 8, 2, P])
        wkT = buf("wkT", [P, 8, P])
        wvT = buf("wvT", [P, 8, P])
        gates = buf("gates", [P, 2])
        loaded, gate_in = sem("fuse_loaded"), sem("gate_in")
        ident_ok, zeroed = sem("ident_ok"), sem("ident_zeroed")
        turned, turned_out = sem("weights_turned"), sem("turned_out")
        fused, fused_hi, fused_lo = sem("fused"), sem("fused_hi"), sem("fused_lo")
        tanh_ok, pad_ok = sem("tanh_ok"), sem("pad_ok")
        bias_in, bias_ok = sem("bias_in"), sem("bias_ok")

        block = ctx.enter_context(nc.Block())

        groups = [(4 * i + par, 4 * i + par + 2) for i in range(4) for par in (0, 1)]

        @block.sync
        def _(sp):
            sp.dma_start(wk[:], io["Wk"]).then_inc(loaded, 16)
            sp.dma_start(wq[:], io["Wq"].rearrange("(k p) n -> p k n", p=P)).then_inc(loaded, 16)
            sp.dma_start(wv[:], io["Wv"]).then_inc(loaded, 16)
            sp.dma_start(wo[:], io["Wo"].rearrange("(c p) n -> p c n", p=P)).then_inc(loaded, 16)
            sp.dma_start(gates[:, 0:1], io["g_xattn"].partition_broadcast(P)).then_inc(gate_in, 16)
            sp.dma_start(gates[:, 1:2], io["g_ffn"].partition_broadcast(P)).then_inc(gate_in, 16)
            sp.dma_start(sb["bo"][:], io["bo"].partition_broadcast(N)).then_inc(bias_in, 16)

        @block.gpsimd
        def _(pool):
            nc.gpsimd.memset(sb["ident"][:], 0.0).then_inc(zeroed, 1)
            pool.wait_ge(zeroed, 1)
            nc.gpsimd.affine_select(out=sb["ident"][:], in_=sb["ident"][:], compare_op=ALU.not_equal, fill=1.0,
                                    base=0, pattern=[[-1, P]], channel_multiplier=1).then_inc(ident_ok, 1)
            for part in ("kvT_hi", "kvT_lo"):
                for b in range(2):
                    nc.gpsimd.memset(sb[part][:, b, M:MW].bitcast(F32), 0.0).then_inc(pad_ok, 1)
            pool.wait_ge(bias_in, 16)
            pool.wait_ge(tanh_ok, 1)
            nc.gpsimd.tensor_scalar(sb["bo"][:], sb["bo"][:], sb["tanh_g"][0:N, 0:1], None, ALU.mult).then_inc(bias_ok, 1)
            pool.wait_ge(bias_ok, 1)
            pool.wait_ge(pad_ok, 4)

        def turn_sources():
            for i in range(2):
                yield wkT[:, 4 * i:4 * i + 4, :], [wk[:, c * P:(c + 1) * P] for c in range(4 * i, 4 * i + 4)]
            for i in range(2):
                yield wvT[:, 4 * i:4 * i + 4, :], [wv[:, c * P:(c + 1) * P] for c in range(4 * i, 4 * i + 4)]
            for i in range(4):
                yield (wqT[:, 2 * i:2 * i + 2, :, :],
                       [wq[:, k, c * P:(c + 1) * P] for c in (2 * i, 2 * i + 1) for k in range(2)])

        @block.tensor
        def _(pe):
            pe.wait_ge(ident_ok, 1)
            pe.wait_ge(loaded, 64)
            for i, (_, srcs) in enumerate(turn_sources()):
                for j, src in enumerate(srcs):
                    last = nc.tensor.transpose(banks[i][:, j * P:(j + 1) * P], src, sb["ident"][:])
                last.then_inc(turned, 1)
            pe.wait_ge(turned_out, 8)
            for i, heads in enumerate(groups):
                for j, h in enumerate(heads):
                    o, c = HD * (h % 2), h // 2
                    for k in range(2):
                        last = nc.tensor.matmul(banks[i][:, (2 * j + k) * P:(2 * j + k + 1) * P],
                                                wqT[o:o + HD, c, k, :], wkT[o:o + HD, c, :], start=True, stop=True)
                last.then_inc(fused, 1)
            for i, heads in enumerate(groups):
                pe.wait_ge(fused_lo, i + 1)
                for j, h in enumerate(heads):
                    o, c = HD * (h % 2), h // 2
                    last = nc.tensor.matmul(banks[i][:, j * D:(j + 1) * D],
                                            wvT[o:o + HD, c, :], wo[o:o + HD, c, :], start=True, stop=True)
                last.then_inc(fused, 1)

        def fused_part(part, i):
            h = groups[i % 8][0]
            return sb[("wqk_" if i < 8 else "wvo_") + part][:, h:h + 3:2, :]

        def fused_bank(i):
            return banks[i % 8][:, :].rearrange("p (h c) -> p h c", h=2)

        @block.scalar
        def _(act):
            act.wait_ge(gate_in, 32)
            nc.scalar.activation(sb["tanh_g"][:], gates[:], ACT.Tanh).then_inc(tanh_ok, 1)
            act.wait_ge(tanh_ok, 1)
            for i in range(16):
                act.wait_ge(fused, i + 1)
                scale = HD ** -0.5 if i < 8 else sb["tanh_g"][:, 0:1]
                nc.scalar.activation(fused_part("hi", i), fused_bank(i), ACT.Copy, scale=scale).then_inc(fused_hi, 1)

        @block.vector
        def _(dve):
            for i, (dst, _) in enumerate(turn_sources()):
                dve.wait_ge(turned, i + 1)
                nc.vector.tensor_copy(dst, banks[i][:, :]).then_inc(turned_out, 1)
            dve.wait_ge(tanh_ok, 1)
            for i in range(16):
                dve.wait_ge(fused_hi, i + 1)
                scale = HD ** -0.5 if i < 8 else sb["tanh_g"][:, 0:1]
                nc.vector.scalar_tensor_tensor(out=fused_part("lo", i), in0=fused_bank(i), scalar=scale,
                                               in1=fused_part("hi", i).bitcast(F32), op0=ALU.mult,
                                               op1=ALU.subtract).then_inc(fused_lo, 1)


def attend(nc, io, sb, banks):
    with ExitStack() as ctx:
        def buf(name, shape, dt=F32):
            return ctx.enter_context(nc.sbuf_tensor(name, shape, dt))

        def sem(name):
            return ctx.enter_context(nc.semaphore(name))

        NB = 8
        x_in = buf("x_in", [N, 2, D])
        x_res = buf("x_res", [N, 2, D])
        xn = buf("xn", [N, 2, D])
        xnT = {q: buf("xnT_" + q, [P, 2, 2 * N], F32R) for q in ("hi", "lo")}
        kv_in = buf("kv_in", [MP, 2, MC * C])
        kv = {q: buf("kv_" + q, [MP, 2, MC * C], F32R) for q in ("hi", "lo")}
        kvT = {q: sb["kvT_" + q] for q in ("hi", "lo")}
        qp = {q: buf("qp_" + q, [P, H, 2 * N], F32R) for q in ("hi", "lo")}
        prob = buf("prob", [N, NB, M])
        pT = {q: buf("pT_" + q, [MP, 2, MC, 4 * N], F32R) for q in ("hi", "lo")}
        zT = {q: buf("zT_" + q, [P, 2, 4 * N], F32R) for q in ("hi", "lo")}
        nmax = buf("nmax", [N, NB])
        psum_ = buf("prob_sum", [N, NB])
        pinv = buf("prob_inv", [N, NB])
        stats = buf("stats", [N, 2, 6])
        mv = buf("mv", [N, 2, 2])
        rs = buf("rs", [N, 4, 2])
        stats2 = buf("stats2", [N, 6])
        mv2 = buf("mv2", [N, 2])
        rs2 = buf("rs2", [N, 4, 2])
        x2 = buf("x2", [N, 2, D])
        hrow = buf("hrow", [N, 2, HW_ROW])

        x_landed = sem("x_landed")
        res_landed = [sem(f"res_landed{b}") for b in range(2)]
        kv_landed = [sem(f"kv_landed{b}") for b in range(2)]
        x_stored = [sem(f"x_stored{b}") for b in range(2)]
        h_stored = [sem(f"h_stored{b}") for b in range(2)]
        res_ready, kv_hi_ready, kv_lo_ready = sem("res_ready"), sem("kv_hi_ready"), sem("kv_lo_ready")
        side_done, side_hi, side_lo = sem("side_done"), sem("side_hi"), sem("side_lo")
        ln_stat, ln_aggr, ln_act, ln_pool = sem("ln_stat"), sem("ln_aggr"), sem("ln_act"), sem("ln_pool")
        x_normed = sem("x_normed")
        ln2_stat, ln2_aggr, ln2_act, ln2_pool = sem("ln2_stat"), sem("ln2_aggr"), sem("ln2_act"), sem("ln2_pool")
        h_ready, x2_ready = sem("h_ready"), sem("x2_ready")
        scores_done, max_ready, exp_done = sem("scores_done"), sem("max_ready"), sem("exp_done")
        inv_ready, norm_dve, norm_act = sem("inv_ready"), sem("norm_dve"), sem("norm_act")
        pT_done, pT_hi, pT_lo = sem("pT_done"), sem("pT_hi"), sem("pT_lo")
        z_done, z_hi, z_lo = sem("z_done"), sem("z_hi"), sem("z_lo")
        z_used = sem("z_used")

        S = banks[0:3]
        T = banks[3:5]
        Z, O, SIDE = banks[5], banks[6], banks[7]
        ident = sb["ident"]

        JOBS = [(3, "q", 4), (7, "q", 5), (9, "q", 6), (11, "q", 7), (13, "kv", 1), (16, "xT", 0), (19, "q", 0),
                (23, "q", 1), (27, "q", 2), (29, "kv", 0), (31, "q", 3)]
        NJ = len(JOBS)
        OWN = 5
        FULL = range(NJ)
        LAST = range(OWN)
        FIRST = range(OWN, NJ)

        def job_index(p, k):
            return NJ * p + k + NJ - OWN

        KV1, XT, KV0 = 4, 5, 9
        Q = {u: k for k, (_, kind, u) in enumerate(JOBS) if kind == "q"}

        def kv_job(p, b):
            return job_index(p, KV1) if b else job_index(p - 1, KV0)

        def back(p, i, per_pair, first):
            if i >= 0:
                return p, i
            return None if first else (p - 1, i + per_pair)

        LN_P, LN2_P = 5, 7

        def second_norm(p, s, first):
            for b in range(2):
                for phase, after in (("add", 0), ("aggr", 1), ("roots", 3), ("apply", 6)):
                    t = H * b + 28 + after
                    if t == s:
                        yield phase, p, b
                    if t - 2 * H == s and not first:
                        yield phase, p - 1, b

        block = ctx.enter_context(nc.Block())

        def body_over_pairs(eng, body):
            body(0, FULL)
            with eng.Fori(1, PAIRS - 1) as p:
                body(p, FULL)
            body(PAIRS - 1, LAST)

        @block.sync
        def _(sp):
            def load_x(p):
                need(sp, x_normed, 2 * p)
                if not isinstance(p, int):
                    apart(sp)
                sp.dma_start(x_in[:], io["x"][bass.ds(2 * p, 2)].rearrange("b n d -> n b d")).then_inc(x_landed, 16)

            def load_kv(p, b):
                bi = 2 * p + b
                if not (isinstance(p, int) and p == 0):
                    need(sp, side_done, kv_job(p - 1, b) + 1)
                    apart(sp)
                need(sp, kv_lo_ready, bi - 1)
                apart(sp)
                src = io["ctx"][bass.ds(bi, 1)].rearrange("b (p c) d -> p (b c d)", c=MC)
                sp.dma_start(kv_in[:, b, :], src).then_inc(kv_landed[b], 16)

            def load_res(p, b):
                bi = 2 * p + b
                need(sp, x2_ready, bi - 1)
                apart(sp)
                src = io["x"][bass.ds(bi, 1)].rearrange("b n d -> n (b d)")
                sp.dma_start(x_res[:, b, :], src).then_inc(res_landed[b], 16)

            def store(bi, b):
                sp.wait_ge(h_ready, 2 * bi + 2)
                apart(sp)
                sp.dma_start(io["x2_rows"][bass.ds(bi * N, N)], x2[:, b, :]).then_inc(x_stored[b], 16)
                sp.dma_start(io["h_rows"][bass.ds(bi * N, N)], hrow[:, b, :]).then_inc(h_stored[b], 16)

            load_x(0)
            load_kv(0, 0)
            load_kv(0, 1)
            load_res(0, 0)
            load_res(0, 1)

            def body(p, jobs):
                first, last = isinstance(p, int) and p == 0, XT not in jobs
                if not last:
                    load_x(p + 1)
                    load_kv(p + 1, 0)
                    load_kv(p + 1, 1)
                if not first:
                    load_res(p, 1)
                    store(2 * p - 1, 1)
                if not last:
                    load_res(p + 1, 0)
                store(2 * p, 0)
            body_over_pairs(sp, body)
            store(B - 1, 1)
            for b in range(2):
                sp.wait_ge(x_stored[b], 16 * PAIRS)
                sp.wait_ge(h_stored[b], 16 * PAIRS)

        @block.gpsimd
        def _(pool):
            def split_context(p, b):
                bi = 2 * p + b
                pool.wait_ge(kv_landed[b], 16 * p + 16)
                need(pool, z_done, 4 * bi - 4)
                apart(pool)
                nc.gpsimd.tensor_copy(kv["hi"][:, b, :], kv_in[:, b, :]).then_inc(kv_hi_ready, 1)
                pool.wait_ge(kv_hi_ready, bi + 1)
                nc.gpsimd.tensor_tensor(kv["lo"][:, b, :], kv_in[:, b, :], kv["hi"][:, b, :].bitcast(F32),
                                        ALU.subtract).then_inc(kv_lo_ready, 1)

            def add_bias(p, b):
                pool.wait_ge(res_landed[b], 16 * p + 16)
                nc.gpsimd.tensor_tensor(x_res[:, b, :], x_res[:, b, :], sb["bo"][:], ALU.add).then_inc(res_ready, 1)

            def newton(r, sem, base):
                nc.gpsimd.tensor_tensor(r[:, 1, :], r[:, 2, :], r[:, 2, :], ALU.mult).then_inc(sem, 1)
                pool.wait_ge(sem, base + 1)
                nc.gpsimd.tensor_tensor(r[:, 1, :], r[:, 1, :], r[:, 0, :], ALU.mult).then_inc(sem, 1)
                pool.wait_ge(sem, base + 2)
                apart(pool)
                nc.gpsimd.tensor_scalar(r[:, 1, :], r[:, 1, :], -0.5, 1.5, ALU.mult, ALU.add).then_inc(sem, 1)
                pool.wait_ge(sem, base + 3)
                nc.gpsimd.tensor_tensor(r[:, 3, :], r[:, 2, :], r[:, 1, :], ALU.mult).then_inc(sem, 1)

            def ln_root(l):
                pool.wait_ge(ln_aggr, 2 * l + 2)
                apart(pool)
                nc.gpsimd.tensor_scalar(rs[:, 0, :], mv[:, :, 1], LN_EPS, None, ALU.add).then_inc(ln_pool, 1)
                pool.wait_ge(ln_act, 2 * l + 2)
                newton(rs, ln_pool, LN_P * l + 1)

            def ln2_root(bi):
                pool.wait_ge(ln2_aggr, bi + 1)
                apart(pool)
                nc.gpsimd.tensor_scalar(rs2[:, 0, 0:1], mv2[:, 1:2], LN_EPS, None, ALU.add).then_inc(ln2_pool, 1)
                nc.gpsimd.tensor_scalar(rs2[:, 0, 1:2], mv2[:, 1:2], 1 + RMS_EPS, LN_EPS * RMS_EPS,
                                        ALU.mult, ALU.add).then_inc(ln2_pool, 1)
                pool.wait_ge(ln2_act, 2 * bi + 2)
                newton(rs2, ln2_pool, LN2_P * bi + 2)
                pool.wait_ge(ln2_pool, LN2_P * bi + 6)
                nc.gpsimd.tensor_tensor(rs2[:, 1, 0:1], rs2[:, 3, 0:1], rs2[:, 0, 1:2], ALU.mult).then_inc(ln2_pool, 1)

            ln_root(0)

            def body(p, jobs):
                first = isinstance(p, int) and p == 0
                split_context(p, 0)
                add_bias(p, 0)
                if XT in jobs:
                    ln_root(p + 1)
                split_context(p, 1)
                if not first:
                    ln2_root(2 * p - 1)
                add_bias(p, 1)
                ln2_root(2 * p)
            body_over_pairs(pool, body)
            ln2_root(B - 1)

        @block.tensor
        def _(pe):
            def three(out, a, b_, start, stop):
                nc.tensor.matmul(out, a[0], b_[0], start=start, stop=False)
                nc.tensor.matmul(out, a[1], b_[0], start=False, stop=False)
                return nc.tensor.matmul(out, a[0], b_[1], start=False, stop=stop)

            def side(p, k):
                _, kind, u = JOBS[k]
                bank = SIDE
                need(pe, side_lo, job_index(p, k))
                if kind == "kv":
                    q = p if u else p + 1
                    pe.wait_ge(kv_landed[u], 16 * q + 16)
                    for c in range(MC):
                        last = nc.tensor.transpose(bank[:, c * MP:(c + 1) * MP], kv_in[:, u, c * C:(c + 1) * C],
                                                   ident[0:MP, 0:MP])
                elif kind == "xT":
                    pe.wait_ge(x_normed, 2 * (p + 1) + 2)
                    for k2 in range(2):
                        for b in range(2):
                            last = nc.tensor.transpose(bank[:, (2 * k2 + b) * N:(2 * k2 + b + 1) * N],
                                                       xn[:, b, k2 * P:(k2 + 1) * P], ident[0:N, 0:N])
                else:
                    if u == 0:
                        pe.wait_ge(side_lo, job_index(p, XT) + 1)
                    for j in range(2):
                        h = 2 * u + j
                        for k2 in range(2):
                            last = three(bank[:, j * 2 * N:(j + 1) * 2 * N],
                                         [sb["wqk_" + q][:, h, k2 * C:(k2 + 1) * C] for q in ("hi", "lo")],
                                         [xnT[q][:, k2, :] for q in ("hi", "lo")], k2 == 0, k2 == 1)
                last.then_inc(side_done, 1)

            def scores(p, b, h):
                s = H * b + h
                g = 2 * H * p + s
                if b == 0 and h % 2 == 0:
                    k = Q[h // 2]
                    pe.wait_ge(side_lo, job_index(p if k < OWN else p - 1, k) + 1)
                if h == 0:
                    pe.wait_ge(side_lo, kv_job(p, b) + 1)
                need(pe, exp_done, g - 1 if s < 2 else g - 2)
                three(S[s % 3][0:N, 0:MW], [qp[q][:, h, b * N:(b + 1) * N] for q in ("hi", "lo")],
                      [kvT[q][:, b, :] for q in ("hi", "lo")], True, True).then_inc(scores_done, 1)

            def turn(p, s):
                g = 2 * H * p + s
                if s % 2:
                    pe.wait_ge(norm_act, H * p + s // 2 + 1)
                else:
                    pe.wait_ge(norm_dve, H * p + s // 2 + 1)
                need(pe, pT_lo, g - 1)
                for c in range(MC):
                    last = nc.tensor.transpose(T[s % 2][0:MP, c * N:(c + 1) * N], prob[:, s % NB, c * MP:(c + 1) * MP],
                                               ident[0:N, 0:N])
                last.then_inc(pT_done, 1)

            def sums(p, qd, c):
                b = qd // 4
                if c == 0:
                    pe.wait_ge(pT_lo, 2 * H * p + 4 * qd + 4)
                    if qd % 4 == 0:
                        pe.wait_ge(kv_lo_ready, 2 * p + b + 1)
                    need(pe, z_lo, 8 * p + qd)
                last = three(Z[:, 0:4 * N], [kv[q][:, b, c * C:(c + 1) * C] for q in ("hi", "lo")],
                             [pT[q][:, qd % 2, c, :] for q in ("hi", "lo")], c == 0, c == MC - 1)
                if c == MC - 1:
                    last.then_inc(z_done, 1)

            def project(p, qd, j):
                if j == 0:
                    pe.wait_ge(z_lo, 8 * p + qd + 1)
                    if qd % 4 == 0:
                        need(pe, x2_ready, 2 * p + qd // 4)
                h = 4 * (qd % 4) + j
                last = three(O[0:N, 0:D], [zT[q][:, qd % 2, j * N:(j + 1) * N] for q in ("hi", "lo")],
                             [sb["wvo_" + q][:, h, :] for q in ("hi", "lo")], h == 0, h == H - 1)
                if j == 3:
                    last.then_inc(z_used, 1)

            for k in FIRST:
                side(-1, k)

            def body(p, jobs):
                first = isinstance(p, int) and p == 0
                for s in range(2 * H):
                    scores(p, s // H, s % H)
                    if s % 4 < MC and (quad := back(p, s // 4 - 2, 8, first)):
                        sums(*quad, s % 4)
                    for k in jobs:
                        if JOBS[k][0] == s:
                            side(p, k)
                    if head := back(p, s - 3, 2 * H, first):
                        turn(*head)
                    if quad := back(p, s // 4 - 3, 8, first):
                        project(*quad, s % 4)
            body_over_pairs(pe, body)
            last = PAIRS - 1
            for s in range(2 * H, 2 * H + 12):
                if s % 4 < MC and s // 4 - 2 < 8:
                    sums(last, s // 4 - 2, s % 4)
                if s - 3 < 2 * H:
                    turn(last, s - 3)
                project(last, s // 4 - 3, s % 4)

        def steps(p, s):
            return 2 * H * p + s

        @block.scalar
        def _(act):
            def side(p, k):
                _, kind, u = JOBS[k]
                bank = SIDE
                act.wait_ge(side_done, job_index(p, k) + 1)
                if kind == "kv":
                    nc.scalar.copy(kvT["hi"][:, u, 0:M], bank[:, 0:M]).then_inc(side_hi, 1)
                elif kind == "xT":
                    nc.scalar.copy(xnT["hi"][:, :, :], bank[:, 0:4 * N].rearrange("p (k n) -> p k n", k=2)).then_inc(side_hi, 1)
                else:
                    nc.scalar.copy(qp["hi"][:, 2 * u:2 * u + 2, :],
                                   bank[:, 0:4 * N].rearrange("p (h n) -> p h n", h=2)).then_inc(side_hi, 1)

            def exps(p, s):
                g = steps(p, s)
                act.wait_ge(max_ready, g + 1)
                need(act, pT_done, g - NB + 1)
                nc.scalar.activation(prob[:, s % NB, :], S[s % 3][0:N, 0:M], ACT.Exp, bias=nmax[:, s % NB:s % NB + 1],
                                     accum_out=psum_[:, s % NB:s % NB + 1]).then_inc(exp_done, 1)

            def norm(p, s):
                act.wait_ge(inv_ready, steps(p, s) + 1)
                nc.scalar.mul(prob[:, s % NB, :], prob[:, s % NB, :], pinv[:, s % NB:s % NB + 1]).then_inc(norm_act, 1)

            def turned(p, s):
                g = steps(p, s)
                act.wait_ge(pT_done, g + 1)
                need(act, z_done, 8 * p + s // 4 - 1)
                dst = pT["hi"][:, (s // 4) % 2, :, (s % 4) * N:(s % 4 + 1) * N]
                nc.scalar.copy(dst, T[s % 2][0:MP, 0:MC * N].rearrange("p (c n) -> p c n", c=MC)).then_inc(pT_hi, 1)

            def ctx_sums(p, qd):
                act.wait_ge(z_done, 8 * p + qd + 1)
                need(act, z_used, 8 * p + qd - 1)
                nc.scalar.copy(zT["hi"][:, qd % 2, :], Z[:, 0:4 * N]).then_inc(z_hi, 1)

            def ln_roots(l):
                act.wait_ge(ln_pool, LN_P * l + 1)
                nc.scalar.activation(rs[:, 1, :], rs[:, 0, :], ACT.Ln).then_inc(ln_act, 1)
                act.wait_ge(ln_act, 2 * l + 1)
                nc.scalar.activation(rs[:, 2, :], rs[:, 1, :], ACT.Exp, scale=-0.5).then_inc(ln_act, 1)

            def ln2_roots(bi):
                act.wait_ge(ln2_pool, LN2_P * bi + 2)
                nc.scalar.activation(rs2[:, 1, :], rs2[:, 0, :], ACT.Ln).then_inc(ln2_act, 1)
                act.wait_ge(ln2_act, 2 * bi + 1)
                nc.scalar.activation(rs2[:, 2, :], rs2[:, 1, :], ACT.Exp, scale=-0.5).then_inc(ln2_act, 1)

            nc.scalar.preload_act_table_set("natural_log_exp_and_others")
            ln_roots(0)
            for k in FIRST:
                side(-1, k)

            def body(p, jobs):
                first = isinstance(p, int) and p == 0
                nc.scalar.preload_act_table_set("natural_log_exp_and_others")
                for s in range(2 * H):
                    if head := back(p, s - 4, 2 * H, first):
                        turned(*head)
                    exps(p, s)
                    if s % 2 == 0 and (head := back(p, s - 1, 2 * H, first)):
                        norm(*head)
                    if s % 4 == MC - 1 and (quad := back(p, s // 4 - 2, 8, first)):
                        ctx_sums(*quad)
                    for k in jobs:
                        if JOBS[k][0] == s:
                            side(p, k)
                    if s == 7 and XT in jobs:
                        ln_roots(p + 1)
                    for phase, q, b in second_norm(p, s, first):
                        if phase == "roots":
                            ln2_roots(2 * q + b)
            body_over_pairs(act, body)
            last = PAIRS - 1
            turned(last, 2 * H - 4)
            norm(last, 2 * H - 1)
            for s in (3, 2, 1):
                turned(last, 2 * H - s)
            ctx_sums(last, 6)
            ctx_sums(last, 7)
            ln2_roots(B - 1)

        @block.vector
        def _(dve):
            def low(dst, src, hi):
                return nc.vector.tensor_tensor(dst, src, hi.bitcast(F32), ALU.subtract)

            def side(p, k):
                _, kind, u = JOBS[k]
                bank = SIDE
                dve.wait_ge(side_hi, job_index(p, k) + 1)
                if kind == "kv":
                    low(kvT["lo"][:, u, 0:M], bank[:, 0:M], kvT["hi"][:, u, 0:M]).then_inc(side_lo, 1)
                elif kind == "xT":
                    low(xnT["lo"][:, :, :], bank[:, 0:4 * N].rearrange("p (k n) -> p k n", k=2),
                        xnT["hi"][:, :, :]).then_inc(side_lo, 1)
                else:
                    low(qp["lo"][:, 2 * u:2 * u + 2, :], bank[:, 0:4 * N].rearrange("p (h n) -> p h n", h=2),
                        qp["hi"][:, 2 * u:2 * u + 2, :]).then_inc(side_lo, 1)

            def maxima(p, s):
                dve.wait_ge(scores_done, steps(p, s) + 1)
                nc.vector.tensor_reduce(nmax[:, s % NB:s % NB + 1], S[s % 3][0:N, 0:M], AX, ALU.max,
                                        negate=True).then_inc(max_ready, 1)

            def norm(p, s):
                g = steps(p, s)
                dve.wait_ge(exp_done, g + 1)
                nc.vector.reciprocal(pinv[:, s % NB:s % NB + 1], psum_[:, s % NB:s % NB + 1]).then_inc(inv_ready, 1)
                if s % 2 == 0:
                    dve.wait_ge(inv_ready, g + 1)
                    nc.vector.tensor_scalar(prob[:, s % NB, :], prob[:, s % NB, :], pinv[:, s % NB:s % NB + 1], None,
                                            ALU.mult).then_inc(norm_dve, 1)

            def turned(p, s):
                dve.wait_ge(pT_hi, steps(p, s) + 1)
                at = (s // 4) % 2, slice(None), slice((s % 4) * N, (s % 4 + 1) * N)
                low(pT["lo"][(slice(None), *at)], T[s % 2][0:MP, 0:MC * N].rearrange("p (c n) -> p c n", c=MC),
                    pT["hi"][(slice(None), *at)]).then_inc(pT_lo, 1)

            def ctx_sums(p, qd):
                dve.wait_ge(z_hi, 8 * p + qd + 1)
                low(zT["lo"][:, qd % 2, :], Z[:, 0:4 * N], zT["hi"][:, qd % 2, :]).then_inc(z_lo, 1)

            def ln_stats(l):
                dve.wait_ge(x_landed, 16 * l + 16)
                for b in range(2):
                    nc.vector.bn_stats(stats[:, b, :], x_in[:, b, :]).then_inc(ln_stat, 1)

            def ln_aggregate(l):
                dve.wait_ge(ln_stat, 2 * l + 2)
                apart(dve)
                for b in range(2):
                    nc.vector.bn_aggr(mv[:, b, :], stats[:, b, :]).then_inc(ln_aggr, 1)

            def ln_apply(l):
                dve.wait_ge(ln_pool, LN_P * l + LN_P)
                need(dve, side_done, job_index(l - 2, XT) + 1)
                for b in range(2):
                    nc.vector.tensor_scalar(xn[:, b, :], x_in[:, b, :], mv[:, b, 0:1], rs[:, 3, b:b + 1],
                                            ALU.subtract, ALU.mult).then_inc(x_normed, 1)

            def ln2_add(p, b):
                bi = 2 * p + b
                dve.wait_ge(z_used, 4 * bi + 4)
                dve.wait_ge(res_ready, bi + 1)
                need(dve, x_stored[b], 16 * p)
                nc.vector.tensor_tensor(x2[:, b, :], O[0:N, 0:D], x_res[:, b, :], ALU.add).then_inc(x2_ready, 1)

            def ln2_stats(p, b):
                dve.wait_ge(x2_ready, 2 * p + b + 1)
                nc.vector.bn_stats(stats2[:], x2[:, b, :]).then_inc(ln2_stat, 1)

            def ln2_aggregate(p, b):
                dve.wait_ge(ln2_stat, 2 * p + b + 1)
                apart(dve)
                nc.vector.bn_aggr(mv2[:], stats2[:]).then_inc(ln2_aggr, 1)

            def ln2_apply(p, b):
                bi = 2 * p + b
                dve.wait_ge(ln2_pool, LN2_P * bi + LN2_P)
                need(dve, h_stored[b], 16 * p)
                nc.vector.tensor_tensor(hrow[:, b, D:D + 1], rs2[:, 1, 0:1], rs2[:, 3, 1:2], ALU.mult).then_inc(h_ready, 1)
                nc.vector.tensor_scalar(hrow[:, b, 0:D], x2[:, b, :], mv2[:, 0:1], rs2[:, 3, 1:2],
                                        ALU.subtract, ALU.mult).then_inc(h_ready, 1)

            ln_stats(0)
            ln_aggregate(0)
            ln_apply(0)
            for k in FIRST:
                side(-1, k)

            def body(p, jobs):
                first = isinstance(p, int) and p == 0
                for s in range(2 * H):
                    norms = list(second_norm(p, s, first))
                    for phase, q, b in norms:
                        if phase == "add":
                            ln2_add(q, b)
                    maxima(p, s)
                    if head := back(p, s - 1, 2 * H, first):
                        norm(*head)
                    if head := back(p, s - 4, 2 * H, first):
                        turned(*head)
                    if s % 4 == MC - 1 and (quad := back(p, s // 4 - 2, 8, first)):
                        ctx_sums(*quad)
                    for k in jobs:
                        if JOBS[k][0] == s:
                            side(p, k)
                    for phase, q, b in norms:
                        if phase == "add":
                            ln2_stats(q, b)
                        if phase == "aggr":
                            ln2_aggregate(q, b)
                        if phase == "apply":
                            ln2_apply(q, b)
                    if XT in jobs and s == 4:
                        ln_stats(p + 1)
                    if XT in jobs and s == 5:
                        ln_aggregate(p + 1)
                    if XT in jobs and s == 10:
                        ln_apply(p + 1)
            body_over_pairs(dve, body)
            last = PAIRS - 1
            norm(last, 2 * H - 1)
            for s in (4, 3, 2, 1):
                turned(last, 2 * H - s)
            ctx_sums(last, 6)
            ctx_sums(last, 7)
            ln2_apply(last, 0)
            ln2_add(last, 1)
            ln2_stats(last, 1)
            ln2_aggregate(last, 1)
            ln2_apply(last, 1)


SHARED_BUFS = [("ident", [P, P], F32), ("tanh_g", [P, 2], F32), ("bo", [N, D], F32),
               ("kvT_hi", [P, 2, MW], F32R), ("kvT_lo", [P, 2, MW], F32R),
               ("wqk_hi", [P, H, 2 * C], F32R), ("wqk_lo", [P, H, 2 * C], F32R),
               ("wvo_hi", [P, H, D], F32R), ("wvo_lo", [P, H, D], F32R)]

TILES = TOK // P
GROUPS = TILES // 4


def route(nc, io, sb, banks):
    with ExitStack() as ctx:
        def buf(name, shape, dt=F32):
            return ctx.enter_context(nc.sbuf_tensor(name, shape, dt))

        def sem(name):
            return ctx.enter_context(nc.semaphore(name))

        h_in = buf("h_in", [P, 2, 4, HW_ROW])
        rw = buf("rw", [P, 2, E])
        rwp = {q: buf("rw_" + q, [P, 2, E], F32R) for q in ("hi", "lo")}
        hT = {q: sb["hT_" + q] for q in ("hi", "lo")}
        logitT = buf("logitT", [E, 2, 4 * P])
        logit = buf("logit", [P, TILES, E])
        prob = buf("gate_prob", [P, TILES, E])
        tie = buf("tie", [P, TILES, E])
        code_i = buf("code_i", [P, E], I32)
        code = buf("code", [P, E])
        rowmax = buf("rowmax", [P, TILES])
        rowsum = buf("rowsum", [P, TILES])
        top = [buf(f"top{k}", [P, TILES]) for k in range(TOPK)]
        first_code = buf("first_code", [P, TILES])
        pick = [sb[f"pick{k}"] for k in range(TOPK)]
        weight = [sb[f"weight{k}"] for k in range(TOPK)]

        h_landed = [sem(f"rows_landed{b}") for b in range(2)]
        rw_landed, rw_hi_ready, rw_lo_ready = sem("rw_landed"), sem("rw_hi_ready"), sem("rw_lo_ready")
        turned, hT_hi_ready, hT_lo_ready = sem("rows_turned"), sem("hT_hi_ready"), sem("hT_lo_ready")
        lt_done, lt_copied, l_turned, l_ready = sem("lt_done"), sem("lt_copied"), sem("l_turned"), sem("l_ready")
        code_made, step, exp_done = sem("code_made"), sem("route_step"), sem("gate_exp_done")

        def loop_over_groups(eng, body):
            body(0, 0)
            body(1, 1)
            with eng.Fori(1, GROUPS // 2) as i:
                body(2 * i, 0, i)
                body(2 * i + 1, 1, i)
            body(GROUPS - 1, 0)

        block = ctx.enter_context(nc.Block())

        @block.sync
        def _(sp):
            sp.dma_start(rw[:], io["router_w"].rearrange("(k p) e -> p k e", p=P)).then_inc(rw_landed, 16)
            rows = io["h_rows"].rearrange("(g t p) d -> p g t d", p=P, t=4)

            def body(g, b, i=None):
                if i is not None or g > 1:
                    sp.wait_ge(l_ready, g - 1)
                    apart(sp)
                sp.dma_start(h_in[:, b, :, :], rows[:, bass.ds(g, 1), :, :].rearrange("p g t d -> p (g t) d")
                             ).then_inc(h_landed[b], 16)
            loop_over_groups(sp, body)

        @block.gpsimd
        def _(pool):
            nc.gpsimd.iota(code_i[:], pattern=[[-1, E]], base=E, channel_multiplier=0).then_inc(code_made, 1)

        def pairs_before(g, i):
            return g // 2 if i is None else i

        @block.tensor
        def _(pe):
            def turn(g, b, i):
                pe.wait_ge(h_landed[b], 16 * pairs_before(g, i) + 16)
                if i is not None or g > 1:
                    pe.wait_ge(hT_lo_ready, 2 * g - 2)
                for k in range(2):
                    for t in range(4):
                        last = nc.tensor.transpose(banks[2 * b + k][:, t * P:(t + 1) * P], h_in[:, b, t, k * P:(k + 1) * P],
                                                   sb["ident"][:])
                    last.then_inc(turned, 1)

            def logits(g, b):
                pe.wait_ge(hT_lo_ready, 2 * g + 2)
                at = bass.ds(4 * P * g, 4 * P)
                products = [("hi", "hi"), ("lo", "hi"), ("hi", "lo")]
                for n, (k, (w, h)) in enumerate((k, q) for k in range(2) for q in products):
                    last = nc.tensor.matmul(banks[4 + b][0:E, :], rwp[w][:, k, :], hT[h][:, k, at], start=n == 0, stop=n == 5)
                last.then_inc(lt_done, 1)
                pe.wait_ge(lt_copied, g + 1)
                apart(pe)
                for t in range(4):
                    last = nc.tensor.transpose(banks[6 + b][:, t * E:(t + 1) * E], logitT[:, b, t * P:(t + 1) * P],
                                               sb["ident"][0:E, 0:E])
                last.then_inc(l_turned, 1)

            pe.wait_ge(rw_lo_ready, 1)

            def body(g, b, i=None):
                turn(g, b, i)
                if i is not None or g > 0:
                    logits(g - 1, 1 - b)
            loop_over_groups(pe, body)
            logits(GROUPS - 1, 0)

        @block.scalar
        def _(act):
            def body(g, b, i=None):
                for k in range(2):
                    act.wait_ge(turned, 2 * g + k + 1)
                    nc.scalar.copy(hT["hi"][:, k, bass.ds(4 * P * g, 4 * P)], banks[2 * b + k][:, :]).then_inc(hT_hi_ready, 1)
            nc.scalar.preload_act_table_set("natural_log_exp_and_others")
            loop_over_groups(act, body)
            act.wait_ge(step, 2)
            nc.scalar.activation(prob[:], logit[:], ACT.Exp).then_inc(exp_done, 1)

        @block.vector
        def _(dve):
            def logits(g, b):
                dve.wait_ge(lt_done, g + 1)
                if not (isinstance(g, int) and g < 2):
                    dve.wait_ge(l_turned, g - 1)
                nc.vector.tensor_copy(logitT[:, b, :], banks[4 + b][0:E, :]).then_inc(lt_copied, 1)
                dve.wait_ge(l_turned, g + 1)
                apart(dve)
                inv = h_in[:, b, :, D:D + 1].to_broadcast([P, 4, E])
                nc.vector.tensor_tensor(logit[:, bass.ds(4 * g, 4), :],
                                        banks[6 + b][:, 0:4 * E].rearrange("p (t e) -> p t e", e=E), inv, ALU.mult
                                        ).then_inc(l_ready, 1)

            dve.wait_ge(rw_landed, 16)
            nc.vector.tensor_copy(rwp["hi"][:], rw[:]).then_inc(rw_hi_ready, 1)
            dve.wait_ge(rw_hi_ready, 1)
            nc.vector.tensor_tensor(rwp["lo"][:], rw[:], rwp["hi"][:].bitcast(F32), ALU.subtract).then_inc(rw_lo_ready, 1)

            def body(g, b, i=None):
                for k in range(2):
                    at = bass.ds(4 * P * g, 4 * P)
                    dve.wait_ge(hT_hi_ready, 2 * g + k + 1)
                    nc.vector.tensor_tensor(hT["lo"][:, k, at], banks[2 * b + k][:, :], hT["hi"][:, k, at].bitcast(F32),
                                            ALU.subtract).then_inc(hT_lo_ready, 1)
                if i is not None or g > 0:
                    logits(g - 1, 1 - b)
            loop_over_groups(dve, body)
            logits(GROUPS - 1, 0)

            def wide(t):
                return t[:].unsqueeze(2).to_broadcast([P, TILES, E])

            dve.wait_ge(l_ready, GROUPS)
            nc.vector.tensor_reduce(rowmax[:], logit[:], AX, ALU.max).then_inc(step, 1)
            dve.wait_ge(step, 1)
            nc.vector.tensor_tensor(logit[:], logit[:], wide(rowmax), ALU.subtract).then_inc(step, 1)
            dve.wait_ge(exp_done, 1)
            nc.vector.tensor_reduce(rowsum[:], prob[:], AX, ALU.add).then_inc(step, 1)
            dve.wait_ge(code_made, 1)
            nc.vector.tensor_copy(code[:], code_i[:]).then_inc(step, 1)
            dve.wait_ge(step, 4)
            nc.vector.reciprocal(rowsum[:], rowsum[:]).then_inc(step, 1)
            dve.wait_ge(step, 5)
            nc.vector.tensor_tensor(prob[:], prob[:], wide(rowsum), ALU.mult).then_inc(step, 1)
            n = 6
            codes = code[:].unsqueeze(1).to_broadcast([P, TILES, E])
            for k in range(TOPK):
                dve.wait_ge(step, n)
                nc.vector.tensor_reduce(top[k][:], prob[:], AX, ALU.max).then_inc(step, 1)
                dve.wait_ge(step, n + 1)
                nc.vector.tensor_tensor(tie[:], prob[:], wide(top[k]), ALU.is_equal).then_inc(step, 1)
                dve.wait_ge(step, n + 2)
                nc.vector.tensor_tensor(tie[:], tie[:], codes, ALU.mult).then_inc(step, 1)
                dve.wait_ge(step, n + 3)
                nc.vector.tensor_reduce(first_code[:], tie[:], AX, ALU.max).then_inc(step, 1)
                dve.wait_ge(step, n + 4)
                nc.vector.tensor_tensor(pick[k][:], codes, wide(first_code), ALU.is_equal).then_inc(step, 1)
                n += 5
                if k == 0:
                    dve.wait_ge(step, n)
                    nc.vector.scalar_tensor_tensor(out=prob[:], in0=pick[0][:], scalar=-2.0, in1=prob[:], op0=ALU.mult,
                                                   op1=ALU.add).then_inc(step, 1)
                    n += 1
            dve.wait_ge(step, n)
            nc.vector.scalar_tensor_tensor(out=rowsum[:], in0=top[0][:], scalar=TOP_EPS, in1=top[1][:], op0=ALU.add,
                                           op1=ALU.add).then_inc(step, 1)
            dve.wait_ge(step, n + 1)
            nc.vector.reciprocal(rowsum[:], rowsum[:]).then_inc(step, 1)
            dve.wait_ge(step, n + 2)
            for k in range(TOPK):
                nc.vector.scalar_tensor_tensor(out=weight[k][:], in0=top[k][:], scalar=sb["tanh_g"][:, 1:2],
                                               in1=rowsum[:], op0=ALU.mult, op1=ALU.mult).then_inc(step, 1)
            dve.wait_ge(step, n + 4)


def gate_matrix(nc, sb):
    with nc.semaphore("gate_step") as step, nc.sbuf_tensor("gate_part", [P, TILES, E], F32) as part, nc.Block() as block:
        @block.vector
        def _(dve):
            def wide(t):
                return t[:].unsqueeze(2).to_broadcast([P, TILES, E])
            nc.vector.tensor_tensor(sb["gate"][:], sb["pick0"][:], wide(sb["weight0"]), ALU.mult).then_inc(step, 1)
            nc.vector.tensor_tensor(part[:], sb["pick1"][:], wide(sb["weight1"]), ALU.mult).then_inc(step, 1)
            dve.wait_ge(step, 2)
            nc.vector.tensor_tensor(sb["gate"][:], sb["gate"][:], part[:], ALU.add).then_inc(step, 1)
            dve.wait_ge(step, 3)


def expert_pair(nc, io, sb, banks, name, pair, shared):
    with ExitStack() as ctx:
        def buf(what, shape, dt=F32):
            return ctx.enter_context(nc.sbuf_tensor(f"{name}_{what}", shape, dt))

        def sem(what):
            return ctx.enter_context(nc.semaphore(f"{name}_{what}"))

        w1_in = buf("w1_in", [P, 2, HID])
        w2_in = buf("w2_in", [P, 4, D])
        rms = buf("rms", [P, 2, 2])
        w1 = {q: buf("w1_" + q, [P, 2, 2, HID], F32R) for q in ("hi", "lo")}
        w2 = {q: buf("w2_" + q, [P, 2, 4, D], F32R) for q in ("hi", "lo")}
        hs = buf("silu", [P, 2, 4 * P])
        hid = {q: buf("hid_" + q, [P, 2, 4, 4 * P], F32R) for q in ("hi", "lo")}
        hT = {q: sb["hT_" + q] for q in ("hi", "lo")}
        acc = sb["acc"]
        w_landed, rms_landed = sem("w_landed"), sem("rms_landed")
        w_hi, w_lo = sem("w_hi_ready"), sem("w_lo_ready")
        h_done, silu_done, hid_hi, hid_lo = sem("h_done"), sem("silu_done"), sem("hid_hi"), sem("hid_lo")
        o_done, acc_done = sem("o_done"), sem("acc_done")
        suffix = "_s" if shared else ""
        H_BANK, O_BANK = banks[0:4], banks[4:8]

        def loop_over_groups(eng, body):
            body(0)
            with eng.Fori(1, GROUPS) as g:
                body(g)

        block = ctx.enter_context(nc.Block())

        @block.sync
        def _(sp):
            for e in range(2):
                sp.dma_start(rms[:, e, :], io["rms_w" + suffix][2 * pair + e].rearrange("(k p) -> p k", p=P),
                             allow_slow_non_contiguous=True
                             ).then_inc(rms_landed, 16)
            for e in range(2):
                if e:
                    sp.wait_ge(w_lo, 3)
                sp.dma_start(w1_in[:], io["w1" + suffix][2 * pair + e].rearrange("(k p) n -> p k n", p=P)
                             ).then_inc(w_landed, 16)
                sp.dma_start(w2_in[:], io["w2" + suffix][2 * pair + e].rearrange("(j p) n -> p j n", p=P)
                             ).then_inc(w_landed, 16)

        @block.tensor
        def _(pe):
            products = [("hi", "hi"), ("lo", "hi"), ("hi", "lo")]

            def hidden(g, e):
                item = 2 * g + e
                for j in range(4):
                    if not (isinstance(g, int) and item == 0):
                        pe.wait_ge(silu_done, 4 * (item - 1) + j + 1)
                    for n, (k, (w, h)) in enumerate((k, q) for k in range(2) for q in products):
                        last = nc.tensor.matmul(H_BANK[j][:, :], w1[w][:, e, k, j * P:(j + 1) * P],
                                                hT[h][:, k, bass.ds(4 * P * g, 4 * P)], start=n == 0, stop=n == 5)
                    last.then_inc(h_done, 1)

            def output(item, e):
                pe.wait_ge(hid_lo, 4 * item + 4)
                if not (isinstance(item, int) and item < 2):
                    pe.wait_ge(acc_done, 4 * (item - 2) + 4)
                for t in range(4):
                    out = O_BANK[2 * e + t // 2][:, (t % 2) * D:(t % 2 + 1) * D]
                    for n, (j, (h, w)) in enumerate((j, q) for j in range(4) for q in products):
                        last = nc.tensor.matmul(out, hid[h][:, e, j, t * P:(t + 1) * P], w2[w][:, e, j, :],
                                                start=n == 0, stop=n == 11)
                    if t % 2:
                        last.then_inc(o_done, 1)

            pe.wait_ge(w_lo, 6)

            def body(g):
                hidden(g, 0)
                if not (isinstance(g, int) and g == 0):
                    output(2 * g - 1, 1)
                hidden(g, 1)
                output(2 * g, 0)
            loop_over_groups(pe, body)
            output(2 * GROUPS - 1, 1)

        def weight_parts():
            for e in range(2):
                for k in range(2):
                    yield e, {q: w1[q][:, e, k, :] for q in w1}, w1_in[:, k, :], rms[:, e, k:k + 1]
                yield e, {q: w2[q][:, e, :, :] for q in w2}, w2_in[:], sb["tanh_g"][:, 1:2] if shared else 1.0

        @block.scalar
        def _(act):
            act.wait_ge(rms_landed, 32)
            for n, (e, dst, src, scale) in enumerate(weight_parts()):
                act.wait_ge(w_landed, 32 * e + 32)
                nc.scalar.activation(dst["hi"], src, ACT.Copy, scale=scale).then_inc(w_hi, 1)

            def body(g):
                for e in range(2):
                    item = 2 * g + e
                    for j in range(4):
                        act.wait_ge(h_done, 4 * item + j + 1)
                        if not (isinstance(g, int) and 4 * item + j < 2):
                            act.wait_ge(hid_lo, 4 * item + j - 1)
                        nc.scalar.activation(hs[:, j % 2, :], H_BANK[j][:, :], ACT.Silu).then_inc(silu_done, 1)
                        act.wait_ge(silu_done, 4 * item + j + 1)
                        if not (isinstance(g, int) and g == 0):
                            act.wait_ge(o_done, 2 * item - 2)
                        nc.scalar.copy(hid["hi"][:, e, j, :], hs[:, j % 2, :]).then_inc(hid_hi, 1)
            loop_over_groups(act, body)

        @block.vector
        def _(dve):
            for n, (e, dst, src, scale) in enumerate(weight_parts()):
                dve.wait_ge(w_hi, n + 1)
                nc.vector.scalar_tensor_tensor(out=dst["lo"], in0=src, scalar=scale, in1=dst["hi"].bitcast(F32),
                                               op0=ALU.mult, op1=ALU.subtract).then_inc(w_lo, 1)

            def accumulate(item, g, e):
                for t in range(4):
                    dve.wait_ge(o_done, 2 * item + t // 2 + 1)
                    if e:
                        dve.wait_ge(acc_done, 4 * item + t - 3)
                    out = O_BANK[2 * e + t // 2][:, (t % 2) * D:(t % 2 + 1) * D]
                    tile_ = acc[:, bass.ds(4 * g + t, 1), :].rearrange("p t d -> p (t d)")
                    if shared:
                        nc.vector.tensor_tensor(tile_, out, tile_, ALU.add).then_inc(acc_done, 1)
                    else:
                        gate = sb["gate"][:, bass.ds(4 * g + t, 1), 2 * pair + e]
                        apart(dve)
                        nc.vector.scalar_tensor_tensor(out=tile_, in0=out, scalar=gate, in1=tile_, op0=ALU.mult,
                                                       op1=ALU.add).then_inc(acc_done, 1)

            def body(g):
                for e in range(2):
                    item = 2 * g + e
                    if not (isinstance(g, int) and g == 0):
                        accumulate(item - 2, g - 1, e)
                    for j in range(4):
                        dve.wait_ge(hid_hi, 4 * item + j + 1)
                        nc.vector.tensor_tensor(hid["lo"][:, e, j, :], hs[:, j % 2, :],
                                                hid["hi"][:, e, j, :].bitcast(F32), ALU.subtract).then_inc(hid_lo, 1)
            loop_over_groups(dve, body)
            for e in range(2):
                accumulate(2 * GROUPS - 2 + e, GROUPS - 1, e)
            dve.wait_ge(acc_done, 8 * GROUPS)


def load_residual(nc, io, sb):
    with nc.semaphore("residual_landed") as landed, nc.Block() as block:
        @block.sync
        def _(sp):
            sp.dma_start(sb["acc"][:], io["x2_rows"].rearrange("(t p) d -> p t d", p=P)).then_inc(landed, 16)
            sp.wait_ge(landed, 16)


def store_out(nc, io, sb):
    with nc.semaphore("out_stored") as stored, nc.Block() as block:
        @block.sync
        def _(sp):
            sp.dma_start(io["out"].rearrange("(t p) d -> p t d", p=P), sb["acc"][:]).then_inc(stored, 16)
            sp.wait_ge(stored, 16)


def build(nc, io):
    io["x2_rows"] = nc.dram_tensor("x2_rows", (TOK, D), F32).ap()
    io["h_rows"] = nc.dram_tensor("h_rows", (TOK, HW_ROW), F32).ap()
    with ExitStack() as ctx:
        def keep(name, shape, dt=F32):
            return ctx.enter_context(nc.sbuf_tensor("keep_" + name, shape, dt))
        sb = {n: keep(n, s, dt) for n, s, dt in KEPT}
        banks = [ctx.enter_context(nc.psum_tensor(f"bank{i}", [P, 512], F32)) for i in range(8)]
        with ExitStack() as ctx2:
            for n, s, dt in SHARED_BUFS:
                if n not in sb:
                    sb[n] = ctx2.enter_context(nc.sbuf_tensor("attend_" + n, s, dt))
            fuse_weights(nc, io, sb, banks)
            attend(nc, io, sb, banks)
        for n, s, dt in MIX_BUFS:
            sb[n] = keep(n, s, dt)
        mix(nc, io, sb, banks)


def mix(nc, io, sb, banks):
    route(nc, io, sb, banks)
    gate_matrix(nc, sb)
    load_residual(nc, io, sb)
    expert_pair(nc, io, sb, banks, "shared", 0, True)
    for pair in range(E // 2):
        expert_pair(nc, io, sb, banks, f"routed{pair}", pair, False)
    store_out(nc, io, sb)


KEPT = [("ident", [P, P], F32), ("tanh_g", [P, 2], F32)]
MIX_BUFS = [("hT_hi", [P, 2, TOK], F32R), ("hT_lo", [P, 2, TOK], F32R), ("acc", [P, TILES, D], F32),
            ("pick0", [P, TILES, E], F32), ("pick1", [P, TILES, E], F32),
            ("weight0", [P, TILES], F32), ("weight1", [P, TILES], F32), ("gate", [P, TILES, E], F32)]

NAMES = [("x", "x"), ("ctx", "ctx_512"), ("g_xattn", "g_xattn"), ("g_ffn", "g_ffn"), ("Wq", "L0_xattn_Wq"),
         ("Wk", "L0_xattn_Wk"), ("Wv", "L0_xattn_Wv"), ("Wo", "L0_xattn_Wo"), ("bo", "L0_xattn_bo"),
         ("router_w", "L0_ffn_router_w"), ("rms_w", "L0_ffn_rms_w"), ("w1", "L0_ffn_w1"), ("w2", "L0_ffn_w2"),
         ("rms_w_s", "L0_ffn_rms_w_s"), ("w1_s", "L0_ffn_w1_s"), ("w2_s", "L0_ffn_w2_s")]


def kernel(**inputs):
    import concourse.bacc as bacc
    from concourse.bass_utils import run_bass_kernel_spmd

    nc = bacc.Bacc("TRN2", target_bir_lowering=False, num_devices=1)
    arrays, io = {}, {}
    for short, name in NAMES:
        a = np.ascontiguousarray(inputs[name])
        arrays["in_" + short] = a
        io[short] = nc.dram_tensor("in_" + short, a.shape, mybir.dt.from_np(a.dtype), kind="ExternalInput").ap()
    io["out"] = nc.dram_tensor("out", (TOK, D), F32, kind="ExternalOutput").ap()
    build(nc, io)
    r = run_bass_kernel_spmd(nc, [arrays], core_ids=[0])
    return r.results[0]["out"].reshape(B, N, D)
```

```python
from contextlib import ExitStack

import numpy as np

import concourse.bass as bass
from concourse import mybir

ALU = mybir.AluOpType
ACT = mybir.ActivationFunctionType
F32 = mybir.dt.float32
F32R = mybir.dt.float32r
I32 = mybir.dt.int32
U32 = mybir.dt.uint32
AX = mybir.AxisListType.X

P = 128
B, N, D = 32, 112, 256
M, C = 375, 128
MC, MP = 3, 125
MW = M + 1
H, HD = 16, 64
PAIRS = B // 2
HW_ROW = D + 1
E, HID, TOPK, SHARED = 14, 512, 2, 2
TOK = B * N
LN_EPS = 1e-5
RMS_EPS = 1.1920929e-07
TOP_EPS = 1e-9


def need(eng, sem, value):
    if isinstance(value, int) and value <= 0:
        return
    eng.wait_ge(sem, value)


def apart(eng):
    eng.nop(nofuse=True)


def fuse_weights(nc, io, sb, banks):
    with ExitStack() as ctx:
        def buf(name, shape, dt=F32):
            return ctx.enter_context(nc.sbuf_tensor(name, shape, dt))

        def sem(name):
            return ctx.enter_context(nc.semaphore(name))

        wq = buf("wq", [P, 2, H * HD])
        wk = buf("wk", [P, H * HD])
        wv = buf("wv", [P, H * HD])
        wo = buf("wo", [P, 8, D])
        wqT = buf("wqT", [P, 8, 2, P])
        wkT = buf("wkT", [P, 8, P])
        wvT = buf("wvT", [P, 8, P])
        gates = buf("gates", [P, 2])
        loaded, gate_in = sem("fuse_loaded"), sem("gate_in")
        ident_ok, zeroed = sem("ident_ok"), sem("ident_zeroed")
        turned, turned_out = sem("weights_turned"), sem("turned_out")
        fused, fused_hi, fused_lo = sem("fused"), sem("fused_hi"), sem("fused_lo")
        tanh_ok, pad_ok = sem("tanh_ok"), sem("pad_ok")
        bias_in, bias_ok, fill_ok = sem("bias_in"), sem("bias_ok"), sem("fill_ok")

        block = ctx.enter_context(nc.Block())

        groups = [(4 * i + par, 4 * i + par + 2) for i in range(4) for par in (0, 1)]

        @block.sync
        def _(sp):
            sp.dma_start(wk[:], io["Wk"]).then_inc(loaded, 16)
            sp.dma_start(wq[:], io["Wq"].rearrange("(k p) n -> p k n", p=P)).then_inc(loaded, 16)
            sp.dma_start(wv[:], io["Wv"]).then_inc(loaded, 16)
            sp.dma_start(wo[:], io["Wo"].rearrange("(c p) n -> p c n", p=P)).then_inc(loaded, 16)
            sp.dma_start(gates[:, 0:1], io["g_xattn"].partition_broadcast(P)).then_inc(gate_in, 16)
            sp.dma_start(gates[:, 1:2], io["g_ffn"].partition_broadcast(P)).then_inc(gate_in, 16)
            sp.dma_start(sb["bo"][:], io["bo"].partition_broadcast(N)).then_inc(bias_in, 16)

        @block.gpsimd
        def _(pool):
            nc.gpsimd.memset(sb["ident"][:], 0.0).then_inc(zeroed, 1)
            pool.wait_ge(zeroed, 1)
            nc.gpsimd.affine_select(out=sb["ident"][:], in_=sb["ident"][:], compare_op=ALU.not_equal, fill=1.0,
                                    base=0, pattern=[[-1, P]], channel_multiplier=1).then_inc(ident_ok, 1)
            nc.gpsimd.memset(sb["fill"][:], 0.0).then_inc(zeroed, 1)
            pool.wait_ge(zeroed, 2)
            nc.gpsimd.iota(sb["fill"][:, D:D + 1].bitcast(I32), pattern=[[0, 1]], base=TOK, channel_multiplier=1
                           ).then_inc(fill_ok, 1)
            pool.wait_ge(fill_ok, 1)
            for part in ("kvT_hi", "kvT_lo"):
                for b in range(2):
                    nc.gpsimd.memset(sb[part][:, b, M:MW].bitcast(F32), 0.0).then_inc(pad_ok, 1)
            pool.wait_ge(bias_in, 16)
            pool.wait_ge(tanh_ok, 1)
            nc.gpsimd.tensor_scalar(sb["bo"][:], sb["bo"][:], sb["tanh_g"][0:N, 0:1], None, ALU.mult).then_inc(bias_ok, 1)
            pool.wait_ge(bias_ok, 1)
            pool.wait_ge(pad_ok, 4)

        def turn_sources():
            for i in range(2):
                yield wkT[:, 4 * i:4 * i + 4, :], [wk[:, c * P:(c + 1) * P] for c in range(4 * i, 4 * i + 4)]
            for i in range(2):
                yield wvT[:, 4 * i:4 * i + 4, :], [wv[:, c * P:(c + 1) * P] for c in range(4 * i, 4 * i + 4)]
            for i in range(4):
                yield (wqT[:, 2 * i:2 * i + 2, :, :],
                       [wq[:, k, c * P:(c + 1) * P] for c in (2 * i, 2 * i + 1) for k in range(2)])

        @block.tensor
        def _(pe):
            pe.wait_ge(ident_ok, 1)
            pe.wait_ge(loaded, 64)
            for i, (_, srcs) in enumerate(turn_sources()):
                for j, src in enumerate(srcs):
                    last = nc.tensor.transpose(banks[i][:, j * P:(j + 1) * P], src, sb["ident"][:])
                last.then_inc(turned, 1)
            pe.wait_ge(turned_out, 8)
            for i, heads in enumerate(groups):
                for j, h in enumerate(heads):
                    o, c = HD * (h % 2), h // 2
                    for k in range(2):
                        last = nc.tensor.matmul(banks[i][:, (2 * j + k) * P:(2 * j + k + 1) * P],
                                                wqT[o:o + HD, c, k, :], wkT[o:o + HD, c, :], start=True, stop=True)
                last.then_inc(fused, 1)
            for i, heads in enumerate(groups):
                pe.wait_ge(fused_lo, i + 1)
                for j, h in enumerate(heads):
                    o, c = HD * (h % 2), h // 2
                    last = nc.tensor.matmul(banks[i][:, j * D:(j + 1) * D],
                                            wvT[o:o + HD, c, :], wo[o:o + HD, c, :], start=True, stop=True)
                last.then_inc(fused, 1)

        def fused_part(part, i):
            h = groups[i % 8][0]
            return sb[("wqk_" if i < 8 else "wvo_") + part][:, h:h + 3:2, :]

        def fused_bank(i):
            return banks[i % 8][:, :].rearrange("p (h c) -> p h c", h=2)

        @block.scalar
        def _(act):
            act.wait_ge(gate_in, 32)
            nc.scalar.activation(sb["tanh_g"][:], gates[:], ACT.Tanh).then_inc(tanh_ok, 1)
            act.wait_ge(tanh_ok, 1)
            for i in range(16):
                act.wait_ge(fused, i + 1)
                scale = HD ** -0.5 if i < 8 else sb["tanh_g"][:, 0:1]
                nc.scalar.activation(fused_part("hi", i), fused_bank(i), ACT.Copy, scale=scale).then_inc(fused_hi, 1)

        @block.vector
        def _(dve):
            for i, (dst, _) in enumerate(turn_sources()):
                dve.wait_ge(turned, i + 1)
                nc.vector.tensor_copy(dst, banks[i][:, :]).then_inc(turned_out, 1)
            dve.wait_ge(tanh_ok, 1)
            for i in range(16):
                dve.wait_ge(fused_hi, i + 1)
                scale = HD ** -0.5 if i < 8 else sb["tanh_g"][:, 0:1]
                nc.vector.scalar_tensor_tensor(out=fused_part("lo", i), in0=fused_bank(i), scalar=scale,
                                               in1=fused_part("hi", i).bitcast(F32), op0=ALU.mult,
                                               op1=ALU.subtract).then_inc(fused_lo, 1)


def attend(nc, io, sb, banks):
    with ExitStack() as ctx:
        def buf(name, shape, dt=F32):
            return ctx.enter_context(nc.sbuf_tensor(name, shape, dt))

        def sem(name):
            return ctx.enter_context(nc.semaphore(name))

        NB = 8
        x_in = buf("x_in", [N, 2, D])
        x_res = buf("x_res", [N, 2, D])
        xn = buf("xn", [N, 2, D])
        xnT = {q: buf("xnT_" + q, [P, 2, 2 * N], F32R) for q in ("hi", "lo")}
        kv_in = buf("kv_in", [MP, 2, MC * C])
        kv = {q: buf("kv_" + q, [MP, 2, MC * C], F32R) for q in ("hi", "lo")}
        kvT = {q: sb["kvT_" + q] for q in ("hi", "lo")}
        qp = {q: buf("qp_" + q, [P, H, 2 * N], F32R) for q in ("hi", "lo")}
        prob = buf("prob", [N, NB, M])
        pT = {q: buf("pT_" + q, [MP, 2, MC, 4 * N], F32R) for q in ("hi", "lo")}
        zT = {q: buf("zT_" + q, [P, 2, 4 * N], F32R) for q in ("hi", "lo")}
        nmax = buf("nmax", [N, NB])
        psum_ = buf("prob_sum", [N, NB])
        pinv = buf("prob_inv", [N, NB])
        stats = buf("stats", [N, 2, 6])
        mv = buf("mv", [N, 2, 2])
        rs = buf("rs", [N, 4, 2])
        stats2 = buf("stats2", [N, 6])
        mv2 = buf("mv2", [N, 2])
        rs2 = buf("rs2", [N, 4, 2])
        x2 = buf("x2", [N, 2, D])
        hrow = buf("hrow", [N, 2, HW_ROW])

        x_landed, slots_filled = sem("x_landed"), sem("slots_filled")
        res_landed = [sem(f"res_landed{b}") for b in range(2)]
        kv_landed = [sem(f"kv_landed{b}") for b in range(2)]
        x_stored = [sem(f"x_stored{b}") for b in range(2)]
        h_stored = [sem(f"h_stored{b}") for b in range(2)]
        res_ready, kv_hi_ready, kv_lo_ready = sem("res_ready"), sem("kv_hi_ready"), sem("kv_lo_ready")
        side_done, side_hi, side_lo = sem("side_done"), sem("side_hi"), sem("side_lo")
        ln_stat, ln_aggr, ln_act, ln_pool = sem("ln_stat"), sem("ln_aggr"), sem("ln_act"), sem("ln_pool")
        x_normed = sem("x_normed")
        ln2_stat, ln2_aggr, ln2_act, ln2_pool = sem("ln2_stat"), sem("ln2_aggr"), sem("ln2_act"), sem("ln2_pool")
        h_ready, x2_ready = sem("h_ready"), sem("x2_ready")
        scores_done, max_ready, exp_done = sem("scores_done"), sem("max_ready"), sem("exp_done")
        inv_ready, norm_dve, norm_act = sem("inv_ready"), sem("norm_dve"), sem("norm_act")
        pT_done, pT_hi, pT_lo = sem("pT_done"), sem("pT_hi"), sem("pT_lo")
        z_done, z_hi, z_lo = sem("z_done"), sem("z_hi"), sem("z_lo")
        z_used = sem("z_used")

        S = banks[0:3]
        T = banks[3:5]
        Z, O, SIDE = banks[5], banks[6], banks[7]
        ident = sb["ident"]

        JOBS = [(3, "q", 4), (7, "q", 5), (9, "q", 6), (11, "q", 7), (13, "kv", 1), (16, "xT", 0), (19, "q", 0),
                (23, "q", 1), (27, "q", 2), (29, "kv", 0), (31, "q", 3)]
        NJ = len(JOBS)
        OWN = 5
        FULL = range(NJ)
        LAST = range(OWN)
        FIRST = range(OWN, NJ)

        def job_index(p, k):
            return NJ * p + k + NJ - OWN

        KV1, XT, KV0 = 4, 5, 9
        Q = {u: k for k, (_, kind, u) in enumerate(JOBS) if kind == "q"}

        def kv_job(p, b):
            return job_index(p, KV1) if b else job_index(p - 1, KV0)

        def back(p, i, per_pair, first):
            if i >= 0:
                return p, i
            return None if first else (p - 1, i + per_pair)

        LN_P, LN2_P = 5, 7

        def second_norm(p, s, first):
            for b in range(2):
                for phase, after in (("add", 0), ("aggr", 1), ("roots", 3), ("apply", 6)):
                    t = H * b + 29 + after
                    if t == s:
                        yield phase, p, b
                    if t - 2 * H == s and not first:
                        yield phase, p - 1, b

        block = ctx.enter_context(nc.Block())

        def body_over_pairs(eng, body):
            body(0, FULL)
            with eng.Fori(1, PAIRS - 1) as p:
                body(p, FULL)
            body(PAIRS - 1, LAST)

        @block.sync
        def _(sp):
            def load_x(p):
                need(sp, x_normed, 2 * p)
                if not isinstance(p, int):
                    apart(sp)
                sp.dma_start(x_in[:], io["x"][bass.ds(2 * p, 2)].rearrange("b n d -> n b d")).then_inc(x_landed, 16)

            def load_kv(p, b):
                bi = 2 * p + b
                if not (isinstance(p, int) and p == 0):
                    need(sp, side_done, kv_job(p - 1, b) + 1)
                    apart(sp)
                need(sp, kv_lo_ready, bi - 1)
                apart(sp)
                src = io["ctx"][bass.ds(bi, 1)].rearrange("b (p c) d -> p (b c d)", c=MC)
                sp.dma_start(kv_in[:, b, :], src).then_inc(kv_landed[b], 16)

            def load_res(p, b):
                bi = 2 * p + b
                need(sp, x2_ready, bi - 1)
                apart(sp)
                src = io["x"][bass.ds(bi, 1)].rearrange("b n d -> n (b d)")
                sp.dma_start(x_res[:, b, :], src).then_inc(res_landed[b], 16)

            def store(bi, b):
                sp.wait_ge(h_ready, 2 * bi + 2)
                apart(sp)
                sp.dma_start(io["x2_rows"][bass.ds(bi * N, N)], x2[:, b, :]).then_inc(x_stored[b], 16)
                sp.dma_start(io["h_rows"][bass.ds(bi * N, N)], hrow[:, b, :]).then_inc(h_stored[b], 16)

            load_x(0)
            load_kv(0, 0)
            load_kv(0, 1)
            load_res(0, 0)
            load_res(0, 1)
            empty = sb["fill"][:].unsqueeze(1).to_broadcast([P, SLOT_TILES, ROW])
            sp.dma_start(io["sorted"].rearrange("(t p) d -> p t d", p=P), empty).then_inc(slots_filled, 16)

            def body(p, jobs):
                first, last = isinstance(p, int) and p == 0, XT not in jobs
                if not last:
                    load_x(p + 1)
                    load_kv(p + 1, 0)
                    load_kv(p + 1, 1)
                if not first:
                    load_res(p, 1)
                    store(2 * p - 1, 1)
                if not last:
                    load_res(p + 1, 0)
                store(2 * p, 0)
            body_over_pairs(sp, body)
            store(B - 1, 1)
            sp.wait_ge(slots_filled, 16)
            for b in range(2):
                sp.wait_ge(x_stored[b], 16 * PAIRS)
                sp.wait_ge(h_stored[b], 16 * PAIRS)

        @block.gpsimd
        def _(pool):
            def split_context(p, b):
                bi = 2 * p + b
                pool.wait_ge(kv_landed[b], 16 * p + 16)
                need(pool, z_done, 4 * bi - 4)
                apart(pool)
                nc.gpsimd.tensor_copy(kv["hi"][:, b, :], kv_in[:, b, :]).then_inc(kv_hi_ready, 1)
                pool.wait_ge(kv_hi_ready, bi + 1)
                nc.gpsimd.tensor_tensor(kv["lo"][:, b, :], kv_in[:, b, :], kv["hi"][:, b, :].bitcast(F32),
                                        ALU.subtract).then_inc(kv_lo_ready, 1)

            def add_bias(p, b):
                pool.wait_ge(res_landed[b], 16 * p + 16)
                nc.gpsimd.tensor_tensor(x_res[:, b, :], x_res[:, b, :], sb["bo"][:], ALU.add).then_inc(res_ready, 1)

            def newton(r, sem, base):
                nc.gpsimd.tensor_tensor(r[:, 1, :], r[:, 2, :], r[:, 2, :], ALU.mult).then_inc(sem, 1)
                pool.wait_ge(sem, base + 1)
                nc.gpsimd.tensor_tensor(r[:, 1, :], r[:, 1, :], r[:, 0, :], ALU.mult).then_inc(sem, 1)
                pool.wait_ge(sem, base + 2)
                apart(pool)
                nc.gpsimd.tensor_scalar(r[:, 1, :], r[:, 1, :], -0.5, 1.5, ALU.mult, ALU.add).then_inc(sem, 1)
                pool.wait_ge(sem, base + 3)
                nc.gpsimd.tensor_tensor(r[:, 3, :], r[:, 2, :], r[:, 1, :], ALU.mult).then_inc(sem, 1)

            def ln_root(l):
                pool.wait_ge(ln_aggr, 2 * l + 2)
                apart(pool)
                nc.gpsimd.tensor_scalar(rs[:, 0, :], mv[:, :, 1], LN_EPS, None, ALU.add).then_inc(ln_pool, 1)
                pool.wait_ge(ln_act, 2 * l + 2)
                newton(rs, ln_pool, LN_P * l + 1)

            def ln2_root(bi):
                pool.wait_ge(ln2_aggr, bi + 1)
                apart(pool)
                nc.gpsimd.tensor_scalar(rs2[:, 0, 0:1], mv2[:, 1:2], LN_EPS, None, ALU.add).then_inc(ln2_pool, 1)
                nc.gpsimd.tensor_scalar(rs2[:, 0, 1:2], mv2[:, 1:2], 1 + RMS_EPS, LN_EPS * RMS_EPS,
                                        ALU.mult, ALU.add).then_inc(ln2_pool, 1)
                pool.wait_ge(ln2_act, 2 * bi + 2)
                newton(rs2, ln2_pool, LN2_P * bi + 2)
                pool.wait_ge(ln2_pool, LN2_P * bi + 6)
                nc.gpsimd.tensor_tensor(rs2[:, 1, 0:1], rs2[:, 3, 0:1], rs2[:, 0, 1:2], ALU.mult).then_inc(ln2_pool, 1)

            ln_root(0)

            def body(p, jobs):
                first = isinstance(p, int) and p == 0
                split_context(p, 0)
                add_bias(p, 0)
                if XT in jobs:
                    ln_root(p + 1)
                split_context(p, 1)
                if not first:
                    ln2_root(2 * p - 1)
                add_bias(p, 1)
                ln2_root(2 * p)
            body_over_pairs(pool, body)
            ln2_root(B - 1)

        @block.tensor
        def _(pe):
            def three(out, a, b_, start, stop):
                nc.tensor.matmul(out, a[0], b_[0], start=start, stop=False)
                nc.tensor.matmul(out, a[1], b_[0], start=False, stop=False)
                return nc.tensor.matmul(out, a[0], b_[1], start=False, stop=stop)

            def side(p, k):
                _, kind, u = JOBS[k]
                bank = SIDE
                need(pe, side_lo, job_index(p, k))
                if kind == "kv":
                    q = p if u else p + 1
                    pe.wait_ge(kv_landed[u], 16 * q + 16)
                    for c in range(MC):
                        last = nc.tensor.transpose(bank[:, c * MP:(c + 1) * MP], kv_in[:, u, c * C:(c + 1) * C],
                                                   ident[0:MP, 0:MP])
                elif kind == "xT":
                    pe.wait_ge(x_normed, 2 * (p + 1) + 2)
                    for k2 in range(2):
                        for b in range(2):
                            last = nc.tensor.transpose(bank[:, (2 * k2 + b) * N:(2 * k2 + b + 1) * N],
                                                       xn[:, b, k2 * P:(k2 + 1) * P], ident[0:N, 0:N])
                else:
                    if u == 0:
                        pe.wait_ge(side_lo, job_index(p, XT) + 1)
                    for j in range(2):
                        h = 2 * u + j
                        for k2 in range(2):
                            last = three(bank[:, j * 2 * N:(j + 1) * 2 * N],
                                         [sb["wqk_" + q][:, h, k2 * C:(k2 + 1) * C] for q in ("hi", "lo")],
                                         [xnT[q][:, k2, :] for q in ("hi", "lo")], k2 == 0, k2 == 1)
                last.then_inc(side_done, 1)

            def scores(p, b, h):
                s = H * b + h
                g = 2 * H * p + s
                if b == 0 and h % 2 == 0:
                    k = Q[h // 2]
                    pe.wait_ge(side_lo, job_index(p if k < OWN else p - 1, k) + 1)
                if h == 0:
                    pe.wait_ge(side_lo, kv_job(p, b) + 1)
                need(pe, exp_done, g - 1 if s < 2 else g - 2)
                three(S[s % 3][0:N, 0:MW], [qp[q][:, h, b * N:(b + 1) * N] for q in ("hi", "lo")],
                      [kvT[q][:, b, :] for q in ("hi", "lo")], True, True).then_inc(scores_done, 1)

            def turn(p, s):
                g = 2 * H * p + s
                if s % 2:
                    pe.wait_ge(norm_act, H * p + s // 2 + 1)
                else:
                    pe.wait_ge(norm_dve, H * p + s // 2 + 1)
                need(pe, pT_lo, g - 1)
                for c in range(MC):
                    last = nc.tensor.transpose(T[s % 2][0:MP, c * N:(c + 1) * N], prob[:, s % NB, c * MP:(c + 1) * MP],
                                               ident[0:N, 0:N])
                last.then_inc(pT_done, 1)

            def sums(p, qd, c):
                b = qd // 4
                if c == 0:
                    pe.wait_ge(pT_lo, 2 * H * p + 4 * qd + 4)
                    if qd % 4 == 0:
                        pe.wait_ge(kv_lo_ready, 2 * p + b + 1)
                    need(pe, z_lo, 8 * p + qd)
                last = three(Z[:, 0:4 * N], [kv[q][:, b, c * C:(c + 1) * C] for q in ("hi", "lo")],
                             [pT[q][:, qd % 2, c, :] for q in ("hi", "lo")], c == 0, c == MC - 1)
                if c == MC - 1:
                    last.then_inc(z_done, 1)

            def project(p, qd, j):
                if j == 0:
                    pe.wait_ge(z_lo, 8 * p + qd + 1)
                    if qd % 4 == 0:
                        need(pe, x2_ready, 2 * p + qd // 4)
                h = 4 * (qd % 4) + j
                last = three(O[0:N, 0:D], [zT[q][:, qd % 2, j * N:(j + 1) * N] for q in ("hi", "lo")],
                             [sb["wvo_" + q][:, h, :] for q in ("hi", "lo")], h == 0, h == H - 1)
                if j == 3:
                    last.then_inc(z_used, 1)

            for k in FIRST:
                side(-1, k)

            def body(p, jobs):
                first = isinstance(p, int) and p == 0
                for s in range(2 * H):
                    scores(p, s // H, s % H)
                    if (s - 1) % 4 < MC and (quad := back(p, (s - 1) // 4 - 2, 8, first)):
                        sums(*quad, (s - 1) % 4)
                    for k in jobs:
                        if JOBS[k][0] == s:
                            side(p, k)
                    if head := back(p, s - 3, 2 * H, first):
                        turn(*head)
                    if quad := back(p, (s - 1) // 4 - 3, 8, first):
                        project(*quad, (s - 1) % 4)
            body_over_pairs(pe, body)
            last = PAIRS - 1
            for s in range(2 * H, 2 * H + 13):
                if (s - 1) % 4 < MC and (s - 1) // 4 - 2 < 8:
                    sums(last, (s - 1) // 4 - 2, (s - 1) % 4)
                if s - 3 < 2 * H:
                    turn(last, s - 3)
                project(last, (s - 1) // 4 - 3, (s - 1) % 4)

        def steps(p, s):
            return 2 * H * p + s

        @block.scalar
        def _(act):
            def side(p, k):
                _, kind, u = JOBS[k]
                bank = SIDE
                act.wait_ge(side_done, job_index(p, k) + 1)
                if kind == "kv":
                    nc.scalar.copy(kvT["hi"][:, u, 0:M], bank[:, 0:M]).then_inc(side_hi, 1)
                elif kind == "xT":
                    nc.scalar.copy(xnT["hi"][:, :, :], bank[:, 0:4 * N].rearrange("p (k n) -> p k n", k=2)).then_inc(side_hi, 1)
                else:
                    nc.scalar.copy(qp["hi"][:, 2 * u:2 * u + 2, :],
                                   bank[:, 0:4 * N].rearrange("p (h n) -> p h n", h=2)).then_inc(side_hi, 1)

            def exps(p, s):
                g = steps(p, s)
                act.wait_ge(max_ready, g + 1)
                need(act, pT_done, g - NB + 1)
                nc.scalar.activation(prob[:, s % NB, :], S[s % 3][0:N, 0:M], ACT.Exp, bias=nmax[:, s % NB:s % NB + 1],
                                     accum_out=psum_[:, s % NB:s % NB + 1]).then_inc(exp_done, 1)

            def norm(p, s):
                act.wait_ge(inv_ready, steps(p, s) + 1)
                nc.scalar.mul(prob[:, s % NB, :], prob[:, s % NB, :], pinv[:, s % NB:s % NB + 1]).then_inc(norm_act, 1)

            def turned(p, s):
                g = steps(p, s)
                act.wait_ge(pT_done, g + 1)
                need(act, z_done, 8 * p + s // 4 - 1)
                dst = pT["hi"][:, (s // 4) % 2, :, (s % 4) * N:(s % 4 + 1) * N]
                nc.scalar.copy(dst, T[s % 2][0:MP, 0:MC * N].rearrange("p (c n) -> p c n", c=MC)).then_inc(pT_hi, 1)

            def ctx_sums(p, qd):
                act.wait_ge(z_done, 8 * p + qd + 1)
                need(act, z_used, 8 * p + qd - 1)
                nc.scalar.copy(zT["hi"][:, qd % 2, :], Z[:, 0:4 * N]).then_inc(z_hi, 1)

            def ln_roots(l):
                act.wait_ge(ln_pool, LN_P * l + 1)
                nc.scalar.activation(rs[:, 1, :], rs[:, 0, :], ACT.Ln).then_inc(ln_act, 1)
                act.wait_ge(ln_act, 2 * l + 1)
                nc.scalar.activation(rs[:, 2, :], rs[:, 1, :], ACT.Exp, scale=-0.5).then_inc(ln_act, 1)

            def ln2_roots(bi):
                act.wait_ge(ln2_pool, LN2_P * bi + 2)
                nc.scalar.activation(rs2[:, 1, :], rs2[:, 0, :], ACT.Ln).then_inc(ln2_act, 1)
                act.wait_ge(ln2_act, 2 * bi + 1)
                nc.scalar.activation(rs2[:, 2, :], rs2[:, 1, :], ACT.Exp, scale=-0.5).then_inc(ln2_act, 1)

            nc.scalar.preload_act_table_set("natural_log_exp_and_others")
            ln_roots(0)
            for k in FIRST:
                side(-1, k)

            def body(p, jobs):
                first = isinstance(p, int) and p == 0
                nc.scalar.preload_act_table_set("natural_log_exp_and_others")
                for s in range(2 * H):
                    if head := back(p, s - 4, 2 * H, first):
                        turned(*head)
                    exps(p, s)
                    if s % 2 == 0 and (head := back(p, s - 1, 2 * H, first)):
                        norm(*head)
                    if s % 4 == MC and (quad := back(p, s // 4 - 2, 8, first)):
                        ctx_sums(*quad)
                    for k in jobs:
                        if JOBS[k][0] == s:
                            side(p, k)
                    if s == 7 and XT in jobs:
                        ln_roots(p + 1)
                    for phase, q, b in second_norm(p, s, first):
                        if phase == "roots":
                            ln2_roots(2 * q + b)
            body_over_pairs(act, body)
            last = PAIRS - 1
            turned(last, 2 * H - 4)
            norm(last, 2 * H - 1)
            for s in (3, 2, 1):
                turned(last, 2 * H - s)
            ctx_sums(last, 6)
            ln2_roots(B - 2)
            ctx_sums(last, 7)
            ln2_roots(B - 1)

        @block.vector
        def _(dve):
            def low(dst, src, hi):
                return nc.vector.tensor_tensor(dst, src, hi.bitcast(F32), ALU.subtract)

            def side(p, k):
                _, kind, u = JOBS[k]
                bank = SIDE
                dve.wait_ge(side_hi, job_index(p, k) + 1)
                if kind == "kv":
                    low(kvT["lo"][:, u, 0:M], bank[:, 0:M], kvT["hi"][:, u, 0:M]).then_inc(side_lo, 1)
                elif kind == "xT":
                    low(xnT["lo"][:, :, :], bank[:, 0:4 * N].rearrange("p (k n) -> p k n", k=2),
                        xnT["hi"][:, :, :]).then_inc(side_lo, 1)
                else:
                    low(qp["lo"][:, 2 * u:2 * u + 2, :], bank[:, 0:4 * N].rearrange("p (h n) -> p h n", h=2),
                        qp["hi"][:, 2 * u:2 * u + 2, :]).then_inc(side_lo, 1)

            def maxima(p, s):
                dve.wait_ge(scores_done, steps(p, s) + 1)
                nc.vector.tensor_reduce(nmax[:, s % NB:s % NB + 1], S[s % 3][0:N, 0:M], AX, ALU.max,
                                        negate=True).then_inc(max_ready, 1)

            def norm(p, s):
                g = steps(p, s)
                dve.wait_ge(exp_done, g + 1)
                nc.vector.reciprocal(pinv[:, s % NB:s % NB + 1], psum_[:, s % NB:s % NB + 1]).then_inc(inv_ready, 1)
                if s % 2 == 0:
                    dve.wait_ge(inv_ready, g + 1)
                    nc.vector.tensor_scalar(prob[:, s % NB, :], prob[:, s % NB, :], pinv[:, s % NB:s % NB + 1], None,
                                            ALU.mult).then_inc(norm_dve, 1)

            def turned(p, s):
                dve.wait_ge(pT_hi, steps(p, s) + 1)
                at = (s // 4) % 2, slice(None), slice((s % 4) * N, (s % 4 + 1) * N)
                low(pT["lo"][(slice(None), *at)], T[s % 2][0:MP, 0:MC * N].rearrange("p (c n) -> p c n", c=MC),
                    pT["hi"][(slice(None), *at)]).then_inc(pT_lo, 1)

            def ctx_sums(p, qd):
                dve.wait_ge(z_hi, 8 * p + qd + 1)
                low(zT["lo"][:, qd % 2, :], Z[:, 0:4 * N], zT["hi"][:, qd % 2, :]).then_inc(z_lo, 1)

            def ln_stats(l):
                dve.wait_ge(x_landed, 16 * l + 16)
                for b in range(2):
                    nc.vector.bn_stats(stats[:, b, :], x_in[:, b, :]).then_inc(ln_stat, 1)

            def ln_aggregate(l):
                dve.wait_ge(ln_stat, 2 * l + 2)
                apart(dve)
                for b in range(2):
                    nc.vector.bn_aggr(mv[:, b, :], stats[:, b, :]).then_inc(ln_aggr, 1)

            def ln_apply(l):
                dve.wait_ge(ln_pool, LN_P * l + LN_P)
                need(dve, side_done, job_index(l - 2, XT) + 1)
                for b in range(2):
                    nc.vector.tensor_scalar(xn[:, b, :], x_in[:, b, :], mv[:, b, 0:1], rs[:, 3, b:b + 1],
                                            ALU.subtract, ALU.mult).then_inc(x_normed, 1)

            def ln2_add(p, b):
                bi = 2 * p + b
                dve.wait_ge(z_used, 4 * bi + 4)
                dve.wait_ge(res_ready, bi + 1)
                need(dve, x_stored[b], 16 * p)
                nc.vector.tensor_tensor(x2[:, b, :], O[0:N, 0:D], x_res[:, b, :], ALU.add).then_inc(x2_ready, 1)

            def ln2_stats(p, b):
                dve.wait_ge(x2_ready, 2 * p + b + 1)
                nc.vector.bn_stats(stats2[:], x2[:, b, :]).then_inc(ln2_stat, 1)

            def ln2_aggregate(p, b):
                dve.wait_ge(ln2_stat, 2 * p + b + 1)
                apart(dve)
                nc.vector.bn_aggr(mv2[:], stats2[:]).then_inc(ln2_aggr, 1)

            def ln2_apply(p, b):
                bi = 2 * p + b
                dve.wait_ge(ln2_pool, LN2_P * bi + LN2_P)
                need(dve, h_stored[b], 16 * p)
                nc.vector.tensor_tensor(hrow[:, b, D:D + 1], rs2[:, 1, 0:1], rs2[:, 3, 1:2], ALU.mult).then_inc(h_ready, 1)
                nc.vector.tensor_scalar(hrow[:, b, 0:D], x2[:, b, :], mv2[:, 0:1], rs2[:, 3, 1:2],
                                        ALU.subtract, ALU.mult).then_inc(h_ready, 1)

            ln_stats(0)
            ln_aggregate(0)
            ln_apply(0)
            for k in FIRST:
                side(-1, k)

            def body(p, jobs):
                first = isinstance(p, int) and p == 0
                for s in range(2 * H):
                    norms = list(second_norm(p, s, first))
                    for phase, q, b in norms:
                        if phase == "add":
                            ln2_add(q, b)
                    maxima(p, s)
                    if head := back(p, s - 4, 2 * H, first):
                        turned(*head)
                    if head := back(p, s - 1, 2 * H, first):
                        norm(*head)
                    if s % 4 == MC and (quad := back(p, s // 4 - 2, 8, first)):
                        ctx_sums(*quad)
                    for k in jobs:
                        if JOBS[k][0] == s:
                            side(p, k)
                    for phase, q, b in norms:
                        if phase == "add":
                            ln2_stats(q, b)
                        if phase == "aggr":
                            ln2_aggregate(q, b)
                        if phase == "apply":
                            ln2_apply(q, b)
                    if XT in jobs and s == 4:
                        ln_stats(p + 1)
                    if XT in jobs and s == 5:
                        ln_aggregate(p + 1)
                    if XT in jobs and s == 10:
                        ln_apply(p + 1)
            body_over_pairs(dve, body)
            last = PAIRS - 1
            norm(last, 2 * H - 1)
            for s in (4, 3, 2, 1):
                turned(last, 2 * H - s)
            ctx_sums(last, 6)
            ctx_sums(last, 7)
            ln2_apply(last, 0)
            ln2_add(last, 1)
            ln2_stats(last, 1)
            ln2_aggregate(last, 1)
            ln2_apply(last, 1)


SHARED_BUFS = [("ident", [P, P], F32), ("tanh_g", [P, 2], F32), ("bo", [N, D], F32),
               ("kvT_hi", [P, 2, MW], F32R), ("kvT_lo", [P, 2, MW], F32R),
               ("wqk_hi", [P, H, 2 * C], F32R), ("wqk_lo", [P, H, 2 * C], F32R),
               ("wvo_hi", [P, H, D], F32R), ("wvo_lo", [P, H, D], F32R)]

TILES = TOK // P
GROUPS = TILES // 4
SLOT_TILES = (TOK * TOPK + E * (P - 1)) // P
SLOT_TILES += SLOT_TILES % 2
ROW = D + 2
WSIZE = 2 * HID + 4 * D
EARLY = 3


def route(nc, io, sb, banks):
    with ExitStack() as ctx:
        def buf(name, shape, dt=F32):
            return ctx.enter_context(nc.sbuf_tensor(name, shape, dt))

        def sem(name):
            return ctx.enter_context(nc.semaphore(name))

        h_in = buf("h_in", [P, 2, 4, HW_ROW])
        w1_in = buf("w1_in", [P, SHARED, 2, HID])
        w2_in = buf("w2_in", [P, SHARED, 4, D])
        rms_s = buf("rms_s", [P, SHARED, 2])
        rw = buf("rw", [P, 2, E])
        rwp = {q: buf("rw_" + q, [P, 2, E], F32R) for q in ("hi", "lo")}
        hT = {q: sb["hT_" + q] for q in ("hi", "lo")}
        logitT = buf("logitT", [E, 2, 4 * P])
        logit = buf("logit", [P, TILES, E])
        prob = buf("gate_prob", [P, TILES, E])
        tie = buf("tie", [P, TILES, E])
        code_i = buf("code_i", [P, E], I32)
        code = buf("code", [P, E])
        rowmax = buf("rowmax", [P, TILES])
        rowsum = buf("rowsum", [P, TILES])
        top = [buf(f"top{k}", [P, TILES]) for k in range(TOPK)]
        first_code = buf("first_code", [P, TILES])
        pick = [sb[f"pick{k}"] for k in range(TOPK)]
        weight = [sb[f"weight{k}"] for k in range(TOPK)]

        h_landed = [sem(f"rows_landed{b}") for b in range(2)]
        w_landed, rms_landed, w_hi, w_lo = sem("ws_landed"), sem("rms_landed"), sem("ws_hi_ready"), sem("ws_lo_ready")
        rw_landed, rw_hi_ready, rw_lo_ready = sem("rw_landed"), sem("rw_hi_ready"), sem("rw_lo_ready")
        turned, hT_hi_ready, hT_lo_ready = sem("rows_turned"), sem("hT_hi_ready"), sem("hT_lo_ready")
        lt_done, lt_copied, l_turned, l_ready = sem("lt_done"), sem("lt_copied"), sem("l_turned"), sem("l_ready")
        code_made, step, exp_done = sem("code_made"), sem("route_step"), sem("gate_exp_done")

        def loop_over_groups(eng, body):
            body(0, 0)
            body(1, 1)
            with eng.Fori(1, GROUPS // 2) as i:
                body(2 * i, 0, i)
                body(2 * i + 1, 1, i)
            body(GROUPS - 1, 0)

        block = ctx.enter_context(nc.Block())

        @block.sync
        def _(sp):
            sp.dma_start(rw[:], io["router_w"].rearrange("(k p) e -> p k e", p=P)).then_inc(rw_landed, 16)
            rows = io["h_rows"].rearrange("(g t p) d -> p g t d", p=P, t=4)

            def load_weights():
                for e in range(SHARED):
                    sp.dma_start(w1_in[:, e], io["w1_s"][e].rearrange("(k p) n -> p k n", p=P)).then_inc(w_landed, 16)
                    sp.dma_start(w2_in[:, e], io["w2_s"][e].rearrange("(j p) n -> p j n", p=P)).then_inc(w_landed, 16)
                    sp.dma_start(rms_s[:, e, :], io["rms_w_s"][e].rearrange("(k p) -> p k", p=P),
                                 allow_slow_non_contiguous=True).then_inc(rms_landed, 16)
                for k in range(2):
                    sp.dma_start(sb["rms"][:, k, :], io["rms_w"][:, k * P:(k + 1) * P].rearrange("e p -> p e"),
                                 allow_slow_non_contiguous=True).then_inc(rms_landed, 16)

            def body(g, b, i=None):
                if i is not None or g > 1:
                    sp.wait_ge(l_ready, g - 1)
                    apart(sp)
                sp.dma_start(h_in[:, b, :, :], rows[:, bass.ds(g, 1), :, :].rearrange("p g t d -> p (g t) d")
                             ).then_inc(h_landed[b], 16)
                if isinstance(g, int) and g == 1:
                    load_weights()
            loop_over_groups(sp, body)

        @block.gpsimd
        def _(pool):
            nc.gpsimd.iota(code_i[:], pattern=[[-1, E]], base=E, channel_multiplier=0).then_inc(code_made, 1)

        def pairs_before(g, i):
            return g // 2 if i is None else i

        @block.tensor
        def _(pe):
            def turn(g, b, i):
                pe.wait_ge(h_landed[b], 16 * pairs_before(g, i) + 16)
                if i is not None or g > 1:
                    pe.wait_ge(hT_lo_ready, 2 * g - 2)
                for k in range(2):
                    for t in range(4):
                        last = nc.tensor.transpose(banks[2 * b + k][:, t * P:(t + 1) * P], h_in[:, b, t, k * P:(k + 1) * P],
                                                   sb["ident"][:])
                    last.then_inc(turned, 1)

            def logits(g, b):
                pe.wait_ge(hT_lo_ready, 2 * g + 2)
                at = bass.ds(4 * P * g, 4 * P)
                products = [("hi", "hi"), ("lo", "hi"), ("hi", "lo")]
                for n, (k, (w, h)) in enumerate((k, q) for k in range(2) for q in products):
                    last = nc.tensor.matmul(banks[4 + b][0:E, :], rwp[w][:, k, :], hT[h][:, k, at], start=n == 0, stop=n == 5)
                last.then_inc(lt_done, 1)
                pe.wait_ge(lt_copied, g + 1)
                apart(pe)
                for t in range(4):
                    last = nc.tensor.transpose(banks[6 + b][:, t * E:(t + 1) * E], logitT[:, b, t * P:(t + 1) * P],
                                               sb["ident"][0:E, 0:E])
                last.then_inc(l_turned, 1)

            pe.wait_ge(rw_lo_ready, 1)

            def body(g, b, i=None):
                turn(g, b, i)
                if i is not None or g > 0:
                    logits(g - 1, 1 - b)
            loop_over_groups(pe, body)
            logits(GROUPS - 1, 0)

        def weight_parts():
            for e in range(2):
                for k in range(2):
                    yield e, {q: sb["w1s_" + q][:, e, k, :] for q in ("hi", "lo")}, w1_in[:, e, k, :], rms_s[:, e, k:k + 1]
                yield e, {q: sb["w2s_" + q][:, e, :, :] for q in ("hi", "lo")}, w2_in[:, e], sb["tanh_g"][:, 1:2]

        @block.scalar
        def _(act):
            def body(g, b, i=None):
                for k in range(2):
                    act.wait_ge(turned, 2 * g + k + 1)
                    nc.scalar.copy(hT["hi"][:, k, bass.ds(4 * P * g, 4 * P)], banks[2 * b + k][:, :]).then_inc(hT_hi_ready, 1)
            nc.scalar.preload_act_table_set("natural_log_exp_and_others")
            loop_over_groups(act, body)
            act.wait_ge(rms_landed, 64)
            act.wait_ge(w_landed, 64)
            for _, dst, src, scale in weight_parts():
                nc.scalar.activation(dst["hi"], src, ACT.Copy, scale=scale).then_inc(w_hi, 1)
            act.wait_ge(step, 2)
            nc.scalar.activation(prob[:], logit[:], ACT.Exp).then_inc(exp_done, 1)

        @block.vector
        def _(dve):
            def logits(g, b):
                dve.wait_ge(lt_done, g + 1)
                if not (isinstance(g, int) and g < 2):
                    dve.wait_ge(l_turned, g - 1)
                nc.vector.tensor_copy(logitT[:, b, :], banks[4 + b][0:E, :]).then_inc(lt_copied, 1)
                dve.wait_ge(l_turned, g + 1)
                apart(dve)
                inv = h_in[:, b, :, D:D + 1].to_broadcast([P, 4, E])
                nc.vector.tensor_tensor(logit[:, bass.ds(4 * g, 4), :],
                                        banks[6 + b][:, 0:4 * E].rearrange("p (t e) -> p t e", e=E), inv, ALU.mult
                                        ).then_inc(l_ready, 1)

            dve.wait_ge(rw_landed, 16)
            nc.vector.tensor_copy(rwp["hi"][:], rw[:]).then_inc(rw_hi_ready, 1)
            dve.wait_ge(rw_hi_ready, 1)
            nc.vector.tensor_tensor(rwp["lo"][:], rw[:], rwp["hi"][:].bitcast(F32), ALU.subtract).then_inc(rw_lo_ready, 1)

            def body(g, b, i=None):
                for k in range(2):
                    at = bass.ds(4 * P * g, 4 * P)
                    dve.wait_ge(hT_hi_ready, 2 * g + k + 1)
                    nc.vector.tensor_tensor(hT["lo"][:, k, at], banks[2 * b + k][:, :], hT["hi"][:, k, at].bitcast(F32),
                                            ALU.subtract).then_inc(hT_lo_ready, 1)
                if i is not None or g > 0:
                    logits(g - 1, 1 - b)
            loop_over_groups(dve, body)
            logits(GROUPS - 1, 0)

            def wide(t):
                return t[:].unsqueeze(2).to_broadcast([P, TILES, E])

            dve.wait_ge(l_ready, GROUPS)
            nc.vector.tensor_reduce(rowmax[:], logit[:], AX, ALU.max).then_inc(step, 1)
            dve.wait_ge(step, 1)
            nc.vector.tensor_tensor(logit[:], logit[:], wide(rowmax), ALU.subtract).then_inc(step, 1)
            dve.wait_ge(exp_done, 1)
            nc.vector.tensor_reduce(rowsum[:], prob[:], AX, ALU.add).then_inc(step, 1)
            dve.wait_ge(code_made, 1)
            nc.vector.tensor_copy(code[:], code_i[:]).then_inc(step, 1)
            dve.wait_ge(step, 4)
            nc.vector.reciprocal(rowsum[:], rowsum[:]).then_inc(step, 1)
            dve.wait_ge(step, 5)
            nc.vector.tensor_tensor(prob[:], prob[:], wide(rowsum), ALU.mult).then_inc(step, 1)
            n = 6
            codes = code[:].unsqueeze(1).to_broadcast([P, TILES, E])
            for k in range(TOPK):
                dve.wait_ge(step, n)
                nc.vector.tensor_reduce(top[k][:], prob[:], AX, ALU.max).then_inc(step, 1)
                dve.wait_ge(step, n + 1)
                nc.vector.tensor_tensor(tie[:], prob[:], wide(top[k]), ALU.is_equal).then_inc(step, 1)
                dve.wait_ge(step, n + 2)
                nc.vector.tensor_tensor(tie[:], tie[:], codes, ALU.mult).then_inc(step, 1)
                dve.wait_ge(step, n + 3)
                nc.vector.tensor_reduce(first_code[:], tie[:], AX, ALU.max).then_inc(step, 1)
                dve.wait_ge(step, n + 4)
                nc.vector.tensor_tensor(pick[k][:], codes, wide(first_code), ALU.is_equal).then_inc(step, 1)
                n += 5
                if k == 0:
                    dve.wait_ge(step, n)
                    nc.vector.scalar_tensor_tensor(out=prob[:], in0=pick[0][:], scalar=-2.0, in1=prob[:], op0=ALU.mult,
                                                   op1=ALU.add).then_inc(step, 1)
                    n += 1
            dve.wait_ge(step, n)
            nc.vector.scalar_tensor_tensor(out=rowsum[:], in0=top[0][:], scalar=TOP_EPS, in1=top[1][:], op0=ALU.add,
                                           op1=ALU.add).then_inc(step, 1)
            dve.wait_ge(step, n + 1)
            nc.vector.reciprocal(rowsum[:], rowsum[:]).then_inc(step, 1)
            dve.wait_ge(step, n + 2)
            for k in range(TOPK):
                nc.vector.scalar_tensor_tensor(out=weight[k][:], in0=top[k][:], scalar=sb["tanh_g"][:, 1:2],
                                               in1=rowsum[:], op0=ALU.mult, op1=ALU.mult).then_inc(step, 1)
            for m, (_, dst, src, scale) in enumerate(weight_parts()):
                dve.wait_ge(w_hi, m + 1)
                nc.vector.scalar_tensor_tensor(out=dst["lo"], in0=src, scalar=scale, in1=dst["hi"].bitcast(F32),
                                               op0=ALU.mult, op1=ALU.subtract).then_inc(w_lo, 1)
            dve.wait_ge(step, n + 4)
            dve.wait_ge(w_lo, 6)
def plan(nc, io, sb, banks):
    with ExitStack() as ctx:
        def buf(name, shape, dt=F32):
            return ctx.enter_context(nc.sbuf_tensor(name, shape, dt))

        def sem(name):
            return ctx.enter_context(nc.semaphore(name))

        both = buf("both", [P, TILES, E])
        ones = buf("ones", [P, P])
        above = buf("above", [P, P])
        smaller = buf("smaller", [P, E, E])
        scan = [buf(f"scan{i}", [P, TILES, E]) for i in range(2)]
        pos = buf("pos", [P, TILES, E])
        count = buf("count", [P, E])
        count_i = buf("count_i", [P, E], I32)
        tiles = buf("tiles", [P, E])
        weighed = buf("weighed", [P, E, E])
        offset = buf("offset", [P, E])
        slot = buf("slot", [P, TILES, TOPK])
        tile_i = buf("tile_i", [1, SLOT_TILES], I32)
        tile_f = buf("tile_f", [1, SLOT_TILES])
        begun = buf("begun", [1, SLOT_TILES, E])
        owner = buf("owner", [1, SLOT_TILES])
        consts, step, counted, meta_ok = sem("plan_consts"), sem("plan_step"), sem("counted"), sem("meta_ok")

        block = ctx.enter_context(nc.Block())

        @block.gpsimd
        def _(pool):
            nc.gpsimd.memset(ones[:], 1.0).then_inc(consts, 1)
            nc.gpsimd.memset(above[:], 1.0).then_inc(consts, 1)
            pool.wait_ge(consts, 2)
            nc.gpsimd.affine_select(out=above[:], in_=above[:], compare_op=ALU.is_ge, fill=0.0, base=-1,
                                    pattern=[[1, P]], channel_multiplier=-1).then_inc(consts, 1)
            nc.gpsimd.memset(smaller[:], 1.0).then_inc(consts, 1)
            pool.wait_ge(consts, 4)
            nc.gpsimd.affine_select(out=smaller[:], in_=smaller[:], compare_op=ALU.is_ge, fill=0.0, base=-1,
                                    pattern=[[1, E], [-1, E]], channel_multiplier=0).then_inc(consts, 1)
            nc.gpsimd.iota(tile_i[:], pattern=[[1, SLOT_TILES]], base=0, channel_multiplier=0).then_inc(consts, 1)
            for k in range(TOPK):
                nc.gpsimd.iota(sb["meta"][:, :, k, 0].bitcast(I32), pattern=[[P, TILES]], base=0,
                               channel_multiplier=1).then_inc(meta_ok, 1)
            pool.wait_ge(meta_ok, 2)

        @block.tensor
        def _(pe):
            pe.wait_ge(consts, 3)
            pe.wait_ge(step, 1)
            for lhs, bank in ((above, banks[0]), (ones, banks[1])):
                nc.tensor.matmul(bank[:, 0:TILES * E], lhs[:], both[:].rearrange("p t e -> p (t e)"), start=True,
                                 stop=True).then_inc(counted, 1)

        @block.vector
        def _(dve):
            def by_tile(t):
                return t[:].unsqueeze(1).to_broadcast([P, TILES, E])

            nc.vector.tensor_tensor(both[:], sb["pick0"][:], sb["pick1"][:], ALU.add).then_inc(step, 1)
            for k in range(TOPK):
                nc.vector.tensor_copy(sb["meta"][:, :, k, 1], sb[f"weight{k}"][:]).then_inc(step, 1)
            dve.wait_ge(consts, 6)
            nc.vector.tensor_copy(tile_f[:], tile_i[:]).then_inc(step, 1)
            nc.vector.memset(scan[0][:, 0:1, :], 0.0).then_inc(step, 1)
            dve.wait_ge(counted, 2)
            total = banks[1][:, 0:TILES * E].rearrange("p (t e) -> p t e", e=E)
            nc.vector.tensor_copy(scan[0][:, 1:TILES, :], total[:, 0:TILES - 1, :]).then_inc(step, 1)
            nc.vector.tensor_reduce(count[:], total.rearrange("p t e -> p e t"), AX, ALU.add).then_inc(step, 1)
            dve.wait_ge(step, 7)
            nc.vector.tensor_scalar(count[:], count[:], float(P - 1), None, ALU.add).then_inc(step, 1)
            dve.wait_ge(step, 8)
            nc.vector.tensor_copy(count_i[:], count[:]).then_inc(step, 1)
            dve.wait_ge(step, 9)
            nc.vector.tensor_scalar(count_i[:], count_i[:], 7, None, ALU.arith_shift_right).then_inc(step, 1)
            dve.wait_ge(step, 10)
            nc.vector.tensor_copy(tiles[:], count_i[:]).then_inc(step, 1)
            dve.wait_ge(step, 11)
            nc.vector.tensor_tensor(weighed[:], smaller[:], tiles[:].unsqueeze(1).to_broadcast([P, E, E]), ALU.mult
                                    ).then_inc(step, 1)
            dve.wait_ge(step, 12)
            nc.vector.tensor_reduce(offset[:], weighed[:], AX, ALU.add).then_inc(step, 1)
            dve.wait_ge(step, 13)
            nc.vector.tensor_tensor(begun[:], tile_f[:].unsqueeze(2).to_broadcast([1, SLOT_TILES, E]),
                                    offset[0:1, :].unsqueeze(1).to_broadcast([1, SLOT_TILES, E]), ALU.is_ge
                                    ).then_inc(step, 1)
            dve.wait_ge(step, 14)
            nc.vector.tensor_reduce(owner[:], begun[:], AX, ALU.add).then_inc(step, 1)
            dve.wait_ge(step, 15)
            nc.vector.tensor_scalar(owner[:], owner[:], -1.0, None, ALU.add).then_inc(step, 1)
            dve.wait_ge(step, 16)
            nc.vector.tensor_copy(sb["expert_of"][:], owner[:]).then_inc(step, 1)
            n, src = 17, 0
            for shift in (1, 2, 4, 8, 16):
                old, new = scan[src], scan[1 - src]
                dve.wait_ge(step, n)
                nc.vector.tensor_tensor(new[:, shift:, :], old[:, shift:, :], old[:, 0:TILES - shift, :], ALU.add
                                        ).then_inc(step, 1)
                nc.vector.tensor_copy(new[:, 0:shift, :], old[:, 0:shift, :]).then_inc(step, 1)
                n, src = n + 2, 1 - src
            dve.wait_ge(step, n)
            nc.vector.tensor_tensor(pos[:], scan[src][:], banks[0][:, 0:TILES * E].rearrange("p (t e) -> p t e", e=E),
                                    ALU.add).then_inc(step, 1)
            nc.vector.tensor_scalar(offset[:], offset[:], float(P), None, ALU.mult).then_inc(step, 1)
            dve.wait_ge(step, n + 2)
            nc.vector.tensor_tensor(pos[:], pos[:], by_tile(offset), ALU.add).then_inc(step, 1)
            dve.wait_ge(step, n + 3)
            for k in range(TOPK):
                nc.vector.tensor_tensor(scan[k][:], pos[:], sb[f"pick{k}"][:], ALU.mult).then_inc(step, 1)
            for k in range(TOPK):
                dve.wait_ge(step, n + 4 + k)
                nc.vector.tensor_reduce(slot[:, :, k], scan[k][:], AX, ALU.add).then_inc(step, 1)
            dve.wait_ge(step, n + 7)
            nc.vector.tensor_copy(sb["slot"][:], slot[:]).then_inc(step, 1)
            dve.wait_ge(step, n + 8)


def shared_experts(nc, io, sb, banks):
    with ExitStack() as ctx:
        def buf(what, shape, dt=F32):
            return ctx.enter_context(nc.sbuf_tensor("shared_" + what, shape, dt))

        def sem(what):
            return ctx.enter_context(nc.semaphore("shared_" + what))

        w1 = {q: sb["w1s_" + q] for q in ("hi", "lo")}
        w2 = {q: sb["w2s_" + q] for q in ("hi", "lo")}
        hs = buf("silu", [P, 2, 4 * P])
        hid = {q: buf("hid_" + q, [P, 2, 4, 4 * P], F32R) for q in ("hi", "lo")}
        hT = {q: sb["hT_" + q] for q in ("hi", "lo")}
        acc = buf("acc", [P, TILES, D])
        rows = buf("rows", [P, 2, 4, TOPK, ROW])
        h_done, silu_done, hid_hi, hid_lo = sem("h_done"), sem("silu_done"), sem("hid_hi"), sem("hid_lo")
        o_done, acc_done = sem("o_done"), sem("acc_done")
        index = buf("index", [P, 2, 4, TOPK], U32)
        acc_landed, out_stored = sem("acc_landed"), sem("out_stored")
        rows_landed = [sem(f"rows_landed{b}") for b in range(2)]
        rows_sent = [sem(f"rows_sent{b}") for b in range(2)]
        meta_set = sem("meta_set")
        H_BANK, O_BANK = banks[0:4], banks[4:8]

        def loop_over_groups(eng, body):
            body(0)
            with eng.Fori(1, GROUPS) as g:
                body(g)

        block = ctx.enter_context(nc.Block())

        @block.sync
        def _(sp):
            x2 = io["x2_rows"].rearrange("(t p) d -> p t d", p=P)
            h = io["h_rows"].rearrange("(t p) d -> p t d", p=P)
            out = io["out"][0:TOK].rearrange("(t p) d -> p t d", p=P)
            sp.dma_start(acc[:], x2).then_inc(acc_landed, 16)
            sp.dma_start(io["out"][TOK:TOK + P], sb["fill"][:, 0:D]).then_inc(out_stored, 16)

            def load_rows(g, b):
                for k in range(TOPK):
                    sp.dma_start(rows[:, b, :, k, 0:D], h[:, bass.ds(4 * g, 4), 0:D]).then_inc(rows_landed[b], 16)

            load_rows(0, 0)
            load_rows(1, 1)
            load_experts(sp, io, sb, range(EARLY))

            def store_sums(g):
                sp.wait_ge(acc_done, 8 * g + 8)
                sp.dma_start(out[:, bass.ds(4 * g, 4), :], acc[:, bass.ds(4 * g, 4), :]).then_inc(out_stored, 16)

            def more_rows(g, b):
                sp.wait_ge(rows_sent[b], 16 * 8 * (g // 2 + 1))
                load_rows(g + 2, b)
            for g in range(GROUPS):
                if g + 2 < GROUPS:
                    more_rows(g, g % 2)
                store_sums(g)
            sp.wait_ge(out_stored, 16 * (GROUPS + 1))

        @block.gpsimd
        def _(pool):
            def body(g, b, i=None):
                before = g // 2 if i is None else i
                pool.wait_ge(rows_landed[b], 32 * before + 32)
                apart(pool)
                nc.gpsimd.tensor_copy(rows[:, b, :, :, D:ROW], sb["meta"][:, bass.ds(4 * g, 4), :, :]).then_inc(meta_set, 1)
                nc.gpsimd.tensor_copy(index[:, b, :, :], sb["slot"][:, bass.ds(4 * g, 4), :]).then_inc(meta_set, 1)
                pool.wait_ge(meta_set, 2 * g + 2)
                apart(pool)
                for t in range(4):
                    for k in range(TOPK):
                        nc.gpsimd.indirect_dma_start(io["sorted"], bass.IndirectOffsetOnAxis(ap=index[:, b, t, k:k + 1], axis=0),
                                                     rows[:, b, t, k, :], None).then_inc(rows_sent[b], 16)
            body(0, 0)
            body(1, 1)
            with pool.Fori(1, GROUPS // 2) as i:
                body(2 * i, 0, i)
                body(2 * i + 1, 1, i)
            body(GROUPS - 1, 0)
            pool.wait_ge(rows_sent[0], 16 * 8 * 4)
            pool.wait_ge(rows_sent[1], 16 * 8 * 3)

        @block.tensor
        def _(pe):
            products = [("hi", "hi"), ("lo", "hi"), ("hi", "lo")]

            def hidden(g, e):
                item = 2 * g + e
                for j in range(4):
                    if not (isinstance(g, int) and item == 0):
                        pe.wait_ge(silu_done, 4 * (item - 1) + j + 1)
                    for n, (k, (w, h)) in enumerate((k, q) for k in range(2) for q in products):
                        last = nc.tensor.matmul(H_BANK[j][:, :], w1[w][:, e, k, j * P:(j + 1) * P],
                                                hT[h][:, k, bass.ds(4 * P * g, 4 * P)], start=n == 0, stop=n == 5)
                    last.then_inc(h_done, 1)

            def output(item, e):
                pe.wait_ge(hid_lo, 4 * item + 4)
                if not (isinstance(item, int) and item < 2):
                    pe.wait_ge(acc_done, 4 * (item - 2) + 4)
                for t in range(4):
                    out = O_BANK[2 * e + t // 2][:, (t % 2) * D:(t % 2 + 1) * D]
                    for n, (j, (h, w)) in enumerate((j, q) for j in range(4) for q in products):
                        last = nc.tensor.matmul(out, hid[h][:, e, j, t * P:(t + 1) * P], w2[w][:, e, j, :],
                                                start=n == 0, stop=n == 11)
                    if t % 2:
                        last.then_inc(o_done, 1)

            def body(g):
                hidden(g, 0)
                if not (isinstance(g, int) and g == 0):
                    output(2 * g - 1, 1)
                hidden(g, 1)
                output(2 * g, 0)
            loop_over_groups(pe, body)
            output(2 * GROUPS - 1, 1)

        @block.scalar
        def _(act):
            def body(g):
                for e in range(2):
                    item = 2 * g + e
                    for j in range(4):
                        act.wait_ge(h_done, 4 * item + j + 1)
                        if not (isinstance(g, int) and 4 * item + j < 2):
                            act.wait_ge(hid_lo, 4 * item + j - 1)
                        nc.scalar.activation(hs[:, j % 2, :], H_BANK[j][:, :], ACT.Silu).then_inc(silu_done, 1)
                        act.wait_ge(silu_done, 4 * item + j + 1)
                        if not (isinstance(g, int) and g == 0):
                            act.wait_ge(o_done, 2 * item - 2)
                        nc.scalar.copy(hid["hi"][:, e, j, :], hs[:, j % 2, :]).then_inc(hid_hi, 1)
            loop_over_groups(act, body)

        @block.vector
        def _(dve):
            def accumulate(item, g, e):
                for t in range(4):
                    dve.wait_ge(o_done, 2 * item + t // 2 + 1)
                    if e:
                        dve.wait_ge(acc_done, 4 * item + t - 3)
                    out = O_BANK[2 * e + t // 2][:, (t % 2) * D:(t % 2 + 1) * D]
                    tile_ = acc[:, bass.ds(4 * g + t, 1), :].rearrange("p t d -> p (t d)")
                    nc.vector.tensor_tensor(tile_, out, tile_, ALU.add).then_inc(acc_done, 1)

            dve.wait_ge(acc_landed, 16)
            def body(g):
                for e in range(2):
                    item = 2 * g + e
                    if not (isinstance(g, int) and g == 0):
                        accumulate(item - 2, g - 1, e)
                    for j in range(4):
                        dve.wait_ge(hid_hi, 4 * item + j + 1)
                        nc.vector.tensor_tensor(hid["lo"][:, e, j, :], hs[:, j % 2, :],
                                                hid["hi"][:, e, j, :].bitcast(F32), ALU.subtract).then_inc(hid_lo, 1)
            loop_over_groups(dve, body)
            for e in range(2):
                accumulate(2 * GROUPS - 2 + e, GROUPS - 1, e)
            dve.wait_ge(acc_done, 8 * GROUPS)


def load_experts(sp, io, sb, experts):
    for e in experts:
        w = sb["weights"][:, e, :]
        sp.dma_start(w[:, 0:2 * HID].rearrange("p (k n) -> p k n", k=2),
                     io["w1"][e].rearrange("(k p) n -> p k n", p=P)).then_inc(sb["w_landed"][e], 16)
        sp.dma_start(w[:, 2 * HID:].rearrange("p (j n) -> p j n", j=4),
                     io["w2"][e].rearrange("(j p) n -> p j n", p=P)).then_inc(sb["w_landed"][e], 16)


def routed_experts(nc, io, sb, banks):
    with ExitStack() as ctx:
        def buf(name, shape, dt=F32):
            return ctx.enter_context(nc.sbuf_tensor("routed_" + name, shape, dt))

        def sem(name):
            return ctx.enter_context(nc.semaphore("routed_" + name))

        weights, expert_of = sb["weights"], sb["expert_of"]
        meta = buf("meta", [P, SLOT_TILES, 2])
        rms = sb["rms"]
        h_in = buf("h_in", [P, 2, D])
        hT = buf("hT", [P, 2, 2, P])
        hs = buf("silu", [P, 2, HID])
        hidT = buf("hidT", [P, 2, 4, P])
        y = buf("y", [P, 2, D])
        index = buf("index", [P, 2], U32)

        h_landed = [sem(f"h_landed{b}") for b in range(2)]
        meta_landed, w_ready = sem("meta_landed"), sem("w_ready")
        h_turned, hT_ready = sem("h_turned"), sem("hT_ready")
        hid_done, silu_ready, hid_turned, hidT_ready = sem("hid_done"), sem("silu_ready"), sem("hid_turned"), sem("hidT_ready")
        index_set = sem("index_set")
        o_done, y_ready, y_added = sem("o_done"), sem("y_ready"), sem("y_added")
        HT_BANK, H_BANK, T_BANK, O_BANK = banks[0:2], banks[2:4], banks[4:6], banks[6:8]
        rows = io["sorted"].rearrange("(t p) d -> p t d", p=P)

        def loop_over_tiles(eng, body):
            body(0, 0, 0)
            body(1, 1, 0)
            with eng.Fori(1, SLOT_TILES // 2 - 1) as i:
                body(2 * i, 0, i)
                body(2 * i + 1, 1, i)
            body(SLOT_TILES - 2, 0, SLOT_TILES // 2 - 1)
            body(SLOT_TILES - 1, 1, SLOT_TILES // 2 - 1)

        def early(t, n):
            return isinstance(t, int) and t < n

        def final(t, n):
            return isinstance(t, int) and t >= SLOT_TILES - n

        block = ctx.enter_context(nc.Block())

        @block.sync
        def _(sp):
            for b in range(2):
                sp.wait_ge(h_landed[b], 16)
            sp.dma_start(meta[:], rows[:, :, D:ROW]).then_inc(meta_landed, 16)
            for e in range(E):
                sp.wait_ge(sb["w_landed"][e], 32)
                sp.nop(nofuse=True).then_inc(w_ready, 1)
                if EARLY <= e + 1 < E:
                    load_experts(sp, io, sb, [e + 1])

        @block.gpsimd
        def _(pool):
            pool.wait_ge(meta_landed, 16)

            def body(t, b, i):
                nc.gpsimd.tensor_copy(index[:, b:b + 1], meta[:, bass.ds(t, 1), 0].bitcast(U32)).then_inc(index_set, 1)
                pool.wait_ge(index_set, t + 1)
                pool.wait_ge(y_ready, t + 1)
                if not early(t, 1):
                    pool.wait_ge(y_added, 16 * t)
                apart(pool)
                nc.gpsimd.indirect_dma_start(io["out"], bass.IndirectOffsetOnAxis(ap=index[:, b:b + 1], axis=0), y[:, b, :], None,
                                             compute_op=ALU.add).then_inc(y_added, 16)
            loop_over_tiles(pool, body)
            pool.wait_ge(y_added, 16 * SLOT_TILES)

        @block.tensor
        def _(pe):
            def turn_rows(t, b, i):
                pe.wait_ge(h_landed[b], 16 * i + 16)
                if not early(t, 2):
                    pe.wait_ge(hT_ready, 2 * t - 2)
                for k in range(2):
                    last = nc.tensor.transpose(HT_BANK[b][:, k * P:(k + 1) * P], h_in[:, b, k * P:(k + 1) * P],
                                               sb["ident"][:])
                last.then_inc(h_turned, 1)

            def hidden(t, b):
                e = pe.value_load(expert_of[0:1, bass.ds(t, 1)], min_val=0, max_val=E - 1)
                pe.wait_ge(w_ready, e + 1)
                pe.wait_ge(hT_ready, 2 * t + 2)
                if not early(t, 2):
                    pe.wait_ge(silu_ready, t - 1)
                for k in range(2):
                    last = nc.tensor.matmul(H_BANK[b][:, :], hT[:, b, k, :],
                                            weights[:, bass.ds(e, 1), k * HID:(k + 1) * HID].rearrange("p e n -> p (e n)"),
                                            start=k == 0, stop=k == 1)
                last.then_inc(hid_done, 1)
                return e

            def turn_hidden(t, b):
                pe.wait_ge(silu_ready, t + 1)
                if not early(t, 2):
                    pe.wait_ge(hidT_ready, t - 1)
                for j in range(4):
                    last = nc.tensor.transpose(T_BANK[b][:, j * P:(j + 1) * P], hs[:, b, j * P:(j + 1) * P], sb["ident"][:])
                last.then_inc(hid_turned, 1)

            def output(t, b):
                e = pe.value_load(expert_of[0:1, bass.ds(t, 1)], min_val=0, max_val=E - 1)
                pe.wait_ge(hidT_ready, t + 1)
                if not early(t, 2):
                    pe.wait_ge(y_ready, t - 1)
                for j in range(4):
                    at = slice(2 * HID + j * D, 2 * HID + (j + 1) * D)
                    last = nc.tensor.matmul(O_BANK[b][:, 0:D], hidT[:, b, j, :],
                                            weights[:, bass.ds(e, 1), at].rearrange("p e n -> p (e n)"),
                                            start=j == 0, stop=j == 3)
                last.then_inc(o_done, 1)

            def body(t, b, i):
                hidden(t, b)
                if not final(t, 1):
                    turn_rows(t + 1, 1 - b, i + b)
                if not early(t, 1):
                    output(t - 1, 1 - b)
                turn_hidden(t, b)
            turn_rows(0, 0, 0)
            loop_over_tiles(pe, body)
            output(SLOT_TILES - 1, 1)

        @block.scalar
        def _(act):
            def load_rows(t, b):
                act.dma_start(h_in[:, b, :], rows[:, bass.ds(t, 1), 0:D].rearrange("p t d -> p (t d)")).then_inc(h_landed[b], 16)
            load_rows(0, 0)
            load_rows(1, 1)

            def body(t, b, i):
                act.wait_ge(hid_done, t + 1)
                if not early(t, 2):
                    act.wait_ge(hid_turned, t - 1)
                nc.scalar.activation(hs[:, b, :], H_BANK[b][:, :], ACT.Silu).then_inc(silu_ready, 1)
                if not final(t, 2):
                    act.wait_ge(h_turned, t + 1)
                    apart(act)
                    load_rows(t + 2, b)
            loop_over_tiles(act, body)

        @block.vector
        def _(dve):
            def rows_out(t, b):
                e = dve.value_load(expert_of[0:1, bass.ds(t, 1)], min_val=0, max_val=E - 1)
                dve.wait_ge(h_turned, t + 1)
                if not early(t, 2):
                    dve.wait_ge(hid_done, t - 1)
                apart(dve)
                for k in range(2):
                    nc.vector.tensor_scalar(hT[:, b, k, :], HT_BANK[b][:, k * P:(k + 1) * P], rms[:, k, bass.ds(e, 1)],
                                            None, ALU.mult).then_inc(hT_ready, 1)

            def hidden_out(t, b):
                dve.wait_ge(hid_turned, t + 1)
                if not early(t, 2):
                    dve.wait_ge(o_done, t - 1)
                nc.vector.tensor_copy(hidT[:, b, :, :], T_BANK[b][:, :].rearrange("p (j n) -> p j n", j=4)).then_inc(hidT_ready, 1)

            def scale(t, b):
                if early(t, 1):
                    dve.wait_ge(meta_landed, 16)
                dve.wait_ge(o_done, t + 1)
                if not early(t, 2):
                    dve.wait_ge(y_added, 16 * t - 16)
                apart(dve)
                nc.vector.tensor_scalar(y[:, b, :], O_BANK[b][:, 0:D], meta[:, bass.ds(t, 1), 1], None, ALU.mult
                                        ).then_inc(y_ready, 1)

            def body(t, b, i):
                if not final(t, 1):
                    rows_out(t + 1, 1 - b)
                if not early(t, 1):
                    scale(t - 1, 1 - b)
                hidden_out(t, b)
            rows_out(0, 0)
            loop_over_tiles(dve, body)
            scale(SLOT_TILES - 1, 1)


def mix(nc, io, sb, banks):
    with ExitStack() as ctx:
        sb["w_landed"] = [ctx.enter_context(nc.semaphore(f"expert{e}_landed")) for e in range(E)]
        at = EARLY * WSIZE
        for name, shape in (("hT_hi", [P, 2, TOK]), ("hT_lo", [P, 2, TOK]),
                            ("w1s_hi", [P, SHARED, 2, HID]), ("w1s_lo", [P, SHARED, 2, HID]),
                            ("w2s_hi", [P, SHARED, 4, D]), ("w2s_lo", [P, SHARED, 4, D])):
            sb[name] = nc.alloc_sbuf_tensor_at("beside_" + name, shape, F32R, offset=sb["weights_at"] + 4 * at)
            at += int(np.prod(shape[1:]))
        assert at <= E * WSIZE
        route(nc, io, sb, banks)
        plan(nc, io, sb, banks)
        shared_experts(nc, io, sb, banks)
        routed_experts(nc, io, sb, banks)


def scratch(nc, io):
    for name, shape in (("x2_rows", (TOK, D)), ("h_rows", (TOK, HW_ROW)), ("sorted", (SLOT_TILES * P, ROW))):
        if name not in io:
            io[name] = nc.dram_tensor(name, shape, F32).ap()


def build(nc, io):
    scratch(nc, io)
    with ExitStack() as ctx:
        def keep(name, shape, dt=F32):
            return ctx.enter_context(nc.sbuf_tensor("keep_" + name, shape, dt))
        sb = {n: keep(n, s, dt) for n, s, dt in KEPT}
        banks = [ctx.enter_context(nc.psum_tensor(f"bank{i}", [P, 512], F32)) for i in range(8)]
        with ExitStack() as ctx2:
            for n, s, dt in SHARED_BUFS:
                if n not in sb:
                    sb[n] = ctx2.enter_context(nc.sbuf_tensor("attend_" + n, s, dt))
            fuse_weights(nc, io, sb, banks)
            attend(nc, io, sb, banks)
        for n, s, dt in MIX_BUFS:
            sb[n] = keep(n, s, dt)
            if n == "weights":
                sb["weights_at"] = nc.sbuf_base - 4 * E * WSIZE
        mix(nc, io, sb, banks)


KEPT = [("ident", [P, P], F32), ("tanh_g", [P, 2], F32), ("fill", [P, ROW], F32)]
MIX_BUFS = [("weights", [P, E, WSIZE], F32), ("pick0", [P, TILES, E], F32), ("pick1", [P, TILES, E], F32),
            ("rms", [P, 2, E], F32), ("weight0", [P, TILES], F32), ("weight1", [P, TILES], F32), ("meta", [P, TILES, TOPK, 2], F32),
            ("slot", [P, TILES, TOPK], U32), ("expert_of", [1, SLOT_TILES], I32)]

NAMES = [("x", "x"), ("ctx", "ctx_512"), ("g_xattn", "g_xattn"), ("g_ffn", "g_ffn"), ("Wq", "L0_xattn_Wq"),
         ("Wk", "L0_xattn_Wk"), ("Wv", "L0_xattn_Wv"), ("Wo", "L0_xattn_Wo"), ("bo", "L0_xattn_bo"),
         ("router_w", "L0_ffn_router_w"), ("rms_w", "L0_ffn_rms_w"), ("w1", "L0_ffn_w1"), ("w2", "L0_ffn_w2"),
         ("rms_w_s", "L0_ffn_rms_w_s"), ("w1_s", "L0_ffn_w1_s"), ("w2_s", "L0_ffn_w2_s")]


def kernel(**inputs):
    import concourse.bacc as bacc
    from concourse.bass_utils import run_bass_kernel_spmd

    nc = bacc.Bacc("TRN2", target_bir_lowering=False, num_devices=1)
    arrays, io = {}, {}
    for short, name in NAMES:
        a = np.ascontiguousarray(inputs[name])
        arrays["in_" + short] = a
        io[short] = nc.dram_tensor("in_" + short, a.shape, mybir.dt.from_np(a.dtype), kind="ExternalInput").ap()
    io["out"] = nc.dram_tensor("out", (TOK + P, D), F32, kind="ExternalOutput").ap()
    build(nc, io)
    r = run_bass_kernel_spmd(nc, [arrays], core_ids=[0])
    return r.results[0]["out"][0:TOK].reshape(B, N, D)
```
